# Optimizing a Trainium2 kernel written in Bass

```python
import numpy as np
import jax
import jax.numpy as jnp

def _softmax(x, axis=-1):
    return jax.nn.softmax(x, axis=axis)

def _gelu(x):
    return jax.nn.gelu(x, approximate=True)

def _silu(x):
    return jax.nn.silu(x)

def _sigmoid(x):
    return jax.nn.sigmoid(x)

def _layernorm(x, axis=-1, eps=1e-05):
    m = jnp.mean(x, axis=axis, keepdims=True)
    v = jnp.var(x, axis=axis, keepdims=True)
    return (x - m) / jnp.sqrt(v + eps)

def _scatter_add(tgt, idx, src, axis=0):
    return tgt.at[idx].add(src)

def _segment_sum(src, seg, n):
    return jax.ops.segment_sum(src, seg, n)
kernel_name = 'mk_perceiver_d1_seqx_r2_3c20b5'

def setup_inputs(seed: int=0):
    np.random.seed(seed)
    _w = jnp.asarray

    def _rec_inputs():
        import jax
        import jax.numpy as jnp
        _rk = jax.random.key(seed)
        x = 7.22e-05 + 1 * jax.random.normal(jax.random.fold_in(_rk, 1), (32, 32, 512), jnp.float32)
        _lenS = 32 - jax.random.randint(jax.random.fold_in(_rk, 7), (32,), 0, max(1, 32 // 4) + 1, jnp.int32)
        _lenS2 = 257 - jax.random.randint(jax.random.fold_in(_rk, 8), (32,), 0, max(1, 257 // 4) + 1, jnp.int32)
        _ctx_768P = jax.random.normal(jax.random.fold_in(_rk, 11), (32, 16, 384), jnp.float32)
        _ctx_768c = jax.random.dirichlet(jax.random.fold_in(_rk, 511), 0.3 * jnp.ones((16,), jnp.float32), (32, 257))
        _ctx_768t = jnp.einsum('bsk,bkd->bsd', _ctx_768c, _ctx_768P)
        _ctx_768t = _ctx_768t * jax.lax.rsqrt(jnp.mean(jnp.square(_ctx_768t)) + 1e-12) * 0.953939
        ctx_768 = -0.000191848 + 0.999787 * (_ctx_768t + 0.3 * jax.random.normal(jax.random.fold_in(_rk, 611), (32, 257, 384), jnp.float32))
        _validS = jnp.arange(32)[None, :] < _lenS[:, None]
        _validS2 = jnp.arange(257)[None, :] < _lenS2[:, None]
        _causal = jnp.tril(jnp.ones((32, 32), dtype=bool))
        mask_BxS2_bk0 = jnp.logical_not(jnp.broadcast_to(_validS2[:, :], (32, 257)))
        return (x, ctx_768, mask_BxS2_bk0)
    x, ctx_768, mask_BxS2_bk0 = _rec_inputs()

    def _L0_xattn_setup():
        import jax, jax.numpy as jnp
        import numpy as np
        HEADS = 8
        DIM_HEAD = 64
        QUERY_DIM = 512
        CONTEXT_DIM = 384
        INNER = HEADS * DIM_HEAD
        key = jax.random.key(seed)
        ks = jax.random.split(key, 8)
        b, n, j = (4, 1024, 1024)
        x = jax.random.normal(ks[0], (b, n, QUERY_DIM), dtype=jnp.float32)
        context = jax.random.normal(ks[1], (b, j, CONTEXT_DIM), dtype=jnp.float32)
        mask = jax.random.randint(ks[2], (b, j), 0, 2).astype(jnp.bool_)
        W_q = jax.random.normal(ks[3], (QUERY_DIM, INNER), dtype=jnp.float32) / np.sqrt(QUERY_DIM)
        W_k = jax.random.normal(ks[4], (CONTEXT_DIM, INNER), dtype=jnp.float32) / np.sqrt(CONTEXT_DIM)
        W_v = jax.random.normal(ks[5], (CONTEXT_DIM, INNER), dtype=jnp.float32) / np.sqrt(CONTEXT_DIM)
        W_o = jax.random.normal(ks[6], (INNER, QUERY_DIM), dtype=jnp.float32) / np.sqrt(INNER)
        b_o = jax.random.normal(ks[7], (QUERY_DIM,), dtype=jnp.float32) * 0.01
        return {'x': x, 'context': context, 'mask': mask, 'W_q': W_q, 'W_k': W_k, 'W_v': W_v, 'W_o': W_o, 'b_o': b_o}
    _L0_xattn_all = _L0_xattn_setup()
    _L0_xattn_in = {k: v for k, v in _L0_xattn_all.items() if k in ('W_q', 'W_k', 'W_v', 'W_o', 'b_o')}
    del _L0_xattn_all

    def _L0_attn_setup():
        import math
        import jax, jax.numpy as jnp
        import numpy as np
        B, S, D = (2, 1024, 512)
        N_HEADS, D_KV = (16, 64)
        INNER = N_HEADS * D_KV
        NUM_BUCKETS = 32
        MAX_DISTANCE = 128

        def _relative_position_bucket(relative_position, num_buckets=NUM_BUCKETS, max_distance=MAX_DISTANCE):
            nb = num_buckets // 2
            rel_buckets = (relative_position > 0).astype(jnp.int32) * nb
            rp = jnp.abs(relative_position)
            max_exact = nb // 2
            is_small = rp < max_exact
            rp_safe = jnp.maximum(rp, 1)
            rp_if_large = max_exact + (jnp.log(rp_safe.astype(jnp.float32) / max_exact) / math.log(max_distance / max_exact) * (nb - max_exact)).astype(jnp.int32)
            rp_if_large = jnp.minimum(rp_if_large, nb - 1)
            return rel_buckets + jnp.where(is_small, rp, rp_if_large)

        def compute_bias(rel_bias, q_len, k_len):
            ctx = jnp.arange(q_len)[:, None]
            mem = jnp.arange(k_len)[None, :]
            buckets = _relative_position_bucket(mem - ctx)
            values = rel_bias[buckets]
            return jnp.transpose(values, (2, 0, 1))[None]
        key = jax.random.key(seed)
        ks = jax.random.split(key, 6)
        s = 1.0 / math.sqrt(D)
        return {'hidden_states': jax.random.normal(ks[0], (B, S, D), jnp.float32), 'wq': jax.random.normal(ks[1], (D, INNER), jnp.float32) * s, 'wk': jax.random.normal(ks[2], (D, INNER), jnp.float32) * s, 'wv': jax.random.normal(ks[3], (D, INNER), jnp.float32) * s, 'wo': jax.random.normal(ks[4], (INNER, D), jnp.float32) * s, 'rel_bias': jax.random.normal(ks[5], (NUM_BUCKETS, N_HEADS), jnp.float32) * 0.1}
    _L0_attn_all = _L0_attn_setup()
    _L0_attn_in = {k: v for k, v in _L0_attn_all.items() if k in ('wq', 'wk', 'wv', 'wo', 'rel_bias')}
    del _L0_attn_all

    def _L0_ffn_setup():
        import jax, jax.numpy as jnp
        import numpy as np
        E = 16
        F_C = 2.0
        D = 512
        I = 4 * D
        IS = 2 * D
        B, S = (4, 512)
        key = jax.random.key(seed)
        ks = jax.random.split(key, 8)
        w = 0.02
        return {'hidden_states': jax.random.normal(ks[0], (B, S, D), dtype=jnp.float32), 'gate_w': jax.random.normal(ks[1], (E, D), dtype=jnp.float32) * w, 'Wg': jax.random.normal(ks[2], (E, I, D), dtype=jnp.float32) * w, 'Wu': jax.random.normal(ks[3], (E, I, D), dtype=jnp.float32) * w, 'Wd': jax.random.normal(ks[4], (E, D, I), dtype=jnp.float32) * w, 'Sg': jax.random.normal(ks[5], (IS, D), dtype=jnp.float32) * w, 'Su': jax.random.normal(ks[6], (IS, D), dtype=jnp.float32) * w, 'Sd': jax.random.normal(ks[7], (D, IS), dtype=jnp.float32) * w}
    _L0_ffn_all = _L0_ffn_setup()
    _L0_ffn_in = {k: v for k, v in _L0_ffn_all.items() if k in ('gate_w', 'Wg', 'Wu', 'Wd', 'Sg', 'Su', 'Sd')}
    del _L0_ffn_all
    return {'x': x, 'ctx_768': ctx_768, 'mask_BxS2_bk0': mask_BxS2_bk0, 'L0_xattn_W_q': _L0_xattn_in['W_q'], 'L0_xattn_W_k': _L0_xattn_in['W_k'], 'L0_xattn_W_v': _L0_xattn_in['W_v'], 'L0_xattn_W_o': _L0_xattn_in['W_o'], 'L0_xattn_b_o': _L0_xattn_in['b_o'], 'L0_attn_wq': _L0_attn_in['wq'], 'L0_attn_wk': _L0_attn_in['wk'], 'L0_attn_wv': _L0_attn_in['wv'], 'L0_attn_wo': _L0_attn_in['wo'], 'L0_attn_rel_bias': _L0_attn_in['rel_bias'], 'L0_ffn_gate_w': _L0_ffn_in['gate_w'], 'L0_ffn_Wg': _L0_ffn_in['Wg'], 'L0_ffn_Wu': _L0_ffn_in['Wu'], 'L0_ffn_Wd': _L0_ffn_in['Wd'], 'L0_ffn_Sg': _L0_ffn_in['Sg'], 'L0_ffn_Su': _L0_ffn_in['Su'], 'L0_ffn_Sd': _L0_ffn_in['Sd']}

def reference(x, ctx_768, mask_BxS2_bk0, L0_xattn_W_q, L0_xattn_W_k, L0_xattn_W_v, L0_xattn_W_o, L0_xattn_b_o, L0_attn_wq, L0_attn_wk, L0_attn_wv, L0_attn_wo, L0_attn_rel_bias, L0_ffn_gate_w, L0_ffn_Wg, L0_ffn_Wu, L0_ffn_Wd, L0_ffn_Sg, L0_ffn_Su, L0_ffn_Sd):
    import jax
    import jax.numpy as jnp

    def _L0_xattn_ref(x, context, mask, W_q, W_k, W_v, W_o, b_o):
        import jax, jax.numpy as jnp
        import numpy as np
        HEADS = 8
        DIM_HEAD = 64
        QUERY_DIM = 512
        CONTEXT_DIM = 384
        INNER = HEADS * DIM_HEAD
        b, n, _ = x.shape
        j = context.shape[1]
        scale = DIM_HEAD ** (-0.5)
        q = (x @ W_q).reshape(b, n, HEADS, DIM_HEAD)
        k = (context @ W_k).reshape(b, j, HEADS, DIM_HEAD)
        v = (context @ W_v).reshape(b, j, HEADS, DIM_HEAD)
        sim = jnp.einsum('bihd,bjhd->bhij', q, k) * scale
        max_neg = -jnp.finfo(sim.dtype).max
        sim = jnp.where(mask[:, None, None, :], sim, max_neg)
        attn = jax.nn.softmax(sim, axis=-1)
        out = jnp.einsum('bhij,bjhd->bihd', attn, v).reshape(b, n, INNER)
        return out @ W_o + b_o

    def _L0_attn_ref(hidden_states, wq, wk, wv, wo, rel_bias):
        import math
        import jax, jax.numpy as jnp
        import numpy as np
        B, S, D = (2, 1024, 512)
        N_HEADS, D_KV = (16, 64)
        INNER = N_HEADS * D_KV
        NUM_BUCKETS = 32
        MAX_DISTANCE = 128

        def _relative_position_bucket(relative_position, num_buckets=NUM_BUCKETS, max_distance=MAX_DISTANCE):
            nb = num_buckets // 2
            rel_buckets = (relative_position > 0).astype(jnp.int32) * nb
            rp = jnp.abs(relative_position)
            max_exact = nb // 2
            is_small = rp < max_exact
            rp_safe = jnp.maximum(rp, 1)
            rp_if_large = max_exact + (jnp.log(rp_safe.astype(jnp.float32) / max_exact) / math.log(max_distance / max_exact) * (nb - max_exact)).astype(jnp.int32)
            rp_if_large = jnp.minimum(rp_if_large, nb - 1)
            return rel_buckets + jnp.where(is_small, rp, rp_if_large)

        def compute_bias(rel_bias, q_len, k_len):
            ctx = jnp.arange(q_len)[:, None]
            mem = jnp.arange(k_len)[None, :]
            buckets = _relative_position_bucket(mem - ctx)
            values = rel_bias[buckets]
            return jnp.transpose(values, (2, 0, 1))[None]
        b, s, _ = hidden_states.shape

        def shape(x):
            return x.reshape(b, s, N_HEADS, D_KV).transpose(0, 2, 1, 3)
        q = shape(hidden_states @ wq)
        k = shape(hidden_states @ wk)
        v = shape(hidden_states @ wv)
        scores = jnp.einsum('bhqd,bhkd->bhqk', q, k)
        position_bias = compute_bias(rel_bias, s, s)
        scores = scores + position_bias
        attn = jax.nn.softmax(scores.astype(jnp.float32), axis=-1).astype(scores.dtype)
        out = jnp.einsum('bhqk,bhkd->bhqd', attn, v)
        out = out.transpose(0, 2, 1, 3).reshape(b, s, INNER)
        return out @ wo

    def _L0_ffn_ref(hidden_states, gate_w, Wg, Wu, Wd, Sg, Su, Sd):
        import jax, jax.numpy as jnp
        import numpy as np
        E = 16
        F_C = 2.0
        D = 512
        I = 4 * D
        IS = 2 * D
        B, S = (4, 512)
        b, s, d = hidden_states.shape
        T = b * s
        C = int(T * F_C / E)
        flat_x = hidden_states.reshape(T, d)
        logits = flat_x @ gate_w.T
        scores = jax.nn.softmax(logits, axis=-1).T
        topk_weight, topk_idx = jax.lax.top_k(scores, C)
        xg = flat_x[topk_idx]
        g = jnp.einsum('ecd,eid->eci', xg, Wg)
        u = jnp.einsum('ecd,eid->eci', xg, Wu)
        h = jax.nn.gelu(g, approximate=False) * u
        eo = jnp.einsum('eci,edi->ecd', h, Wd)
        eo = eo * topk_weight[..., None]
        flat_out = jnp.zeros_like(flat_x).at[topk_idx.reshape(-1)].add(eo.reshape(-1, d))
        out = flat_out.reshape(b, s, d)
        sg = hidden_states @ Sg.T
        su = hidden_states @ Su.T
        shared = jax.nn.gelu(sg, approximate=False) * su @ Sd.T
        return out + shared
    x = x + _L0_xattn_ref(_layernorm(x, axis=-1), ctx_768, mask_BxS2_bk0, L0_xattn_W_q, L0_xattn_W_k, L0_xattn_W_v, L0_xattn_W_o, L0_xattn_b_o)
    x = x + _L0_attn_ref(_layernorm(x, axis=-1), L0_attn_wq, L0_attn_wk, L0_attn_wv, L0_attn_wo, L0_attn_rel_bias)
    x = x + _L0_ffn_ref(_layernorm(x, axis=-1), L0_ffn_gate_w, L0_ffn_Wg, L0_ffn_Wu, L0_ffn_Wd, L0_ffn_Sg, L0_ffn_Su, L0_ffn_Sd)
    return x

_drawn_inputs = setup_inputs


def setup_inputs(seed=0):
    import zlib

    import numpy as np

    out = dict(_drawn_inputs(seed))
    spreads = {}
    factors = {'L0_xattn_b_o': 3.551,
     'L0_attn_rel_bias': 2.871,
     'L0_ffn_gate_w': 5.111,
     'L0_ffn_Wg': 4.626,
     'L0_ffn_Wu': 4.448,
     'L0_ffn_Wd': 4.42,
     'L0_ffn_Sg': 5.639,
     'L0_ffn_Su': 5.468,
     'L0_ffn_Sd': 5.418}
    for name, (base, spread) in spreads.items():
        noise = np.random.default_rng([zlib.crc32(name.encode()), seed]).standard_normal(out[name].shape)
        drawn = base * np.exp(spread * noise) if base else spread * noise
        out[name] = jnp.asarray(drawn.astype(out[name].dtype))
    for name, factor in factors.items():
        out[name] = (out[name] * factor).astype(out[name].dtype)
    return out
```

```python
import math
from contextlib import contextmanager

import numpy as np

import concourse.bass as bass
from concourse import mybir

ALU = mybir.AluOpType
ACT = mybir.ActivationFunctionType
F32 = mybir.dt.float32
F32R = mybir.dt.float32r
U32 = mybir.dt.uint32
U8 = mybir.dt.uint8
AX_X = mybir.AxisListType.X

P = 128
B, S, D = 32, 32, 512
T = B * S
G = T // P
BPG = P // S
KD = D // P
J, CD = 257, 384
KC = CD // P
JE = J + 1
JB = J // P
XH, DH = 8, 64
XP = XH * DH // P
SH = 16
NP = SH * DH // P
NBUCKET = 32
E, C, I = 16, 128, 2048
NI = I // 512
IS = 1024
KI = IS // P
EPS = 1e-5
FLT_MAX = 3.4028234663852886e38


def products(pe, out, stationary, moving, start, stop):
    (wh, wl), (xh, xl) = stationary, moving
    pe.matmul(out, wl, xh, start=start, stop=False)
    pe.matmul(out, wh, xl, start=False, stop=False)
    return pe.matmul(out, wh, xh, start=False, stop=stop)


class Map:

    def __init__(self, nc, offset):
        self.nc, self.offset = nc, offset

    def __call__(self, name, shape, dtype, size=4):
        t = self.nc.alloc_sbuf_tensor_at(name, shape, dtype, offset=self.offset)
        self.offset += (int(np.prod(shape[1:])) * size + 31) // 32 * 32
        return t


@contextmanager
def semaphores(nc, prefix):
    taken = []

    def semaphore(name):
        taken.append(nc.alloc_semaphore(name=prefix + name))
        return taken[-1]

    yield semaphore
    nc.clear_and_free_semaphores(taken)
    nc.all_engine_barrier()


def steps(engine, count, step):
    step(0)
    with engine.Fori(1, count) as i:
        step(i)
SBUF_END = 229344


def cross_attention(nc, ps, x_dram, ctxT, ctx, mask, wq, wkT, wv, wo, bo, ident_dram, rows_dram, x, ident, free):
    sb = Map(nc, free)
    wqh, wql = sb("wqh", [P, KD, D], F32R), sb("wql", [P, KD, D], F32R)
    wkh, wkl = sb("wkh", [P, XP, CD], F32R), sb("wkl", [P, XP, CD], F32R)
    wvh, wvl = sb("wvh", [P, KC, D], F32R), sb("wvl", [P, KC, D], F32R)
    woh, wol = sb("woh", [P, XP, D], F32R), sb("wol", [P, XP, D], F32R)
    raw = Map(nc, sb.offset)
    wq_raw, wk_raw = raw("wq_raw", [P, KD, D], F32), raw("wk_raw", [P, XP, CD], F32)
    wv_raw, wo_raw = raw("wv_raw", [P, KC, D], F32), raw("wo_raw", [P, XP, D], F32)
    qkh, qkl = sb("qkh", [P, KC, 2, BPG, XP, S], F32R), sb("qkl", [P, KC, 2, BPG, XP, S], F32R)
    oh, ol = sb("oh", [P, KC, 2 * XP, P], F32R), sb("ol", [P, KC, 2 * XP, P], F32R)
    xn = sb("xn", [P, D], F32)
    xth, xtl = sb("xth", [P, KD, P], F32R), sb("xtl", [P, KD, P], F32R)
    qh, ql = sb("qh", [P, XP, P], F32R), sb("ql", [P, XP, P], F32R)
    aoh, aol = sb("aoh", [P, XP, P], F32R), sb("aol", [P, XP, P], F32R)
    ctxT_raw, ctx_raw = sb("ctxT_raw", [P, 2, KC, J], F32), sb("ctx_raw", [P, 2, JB, CD], F32)
    last_raw, last_hi = sb("last_raw", [4, 2, CD], F32), sb("last_hi", [4, CD], F32R)
    cTh, cTl = sb("cTh", [P, 2, KC, JE], F32R), sb("cTl", [P, 2, KC, JE], F32R)
    ch, cl = sb("ch", [P, 2, JB, CD], F32R), sb("cl", [P, 2, JB, CD], F32R)
    last4 = sb("last4", [P, 2, CD], F32R)
    mask_all = sb("mask_all", [P, B * J], U8, 1)
    mask_bias = sb("mask_bias", [P, J], F32)
    prob = sb("prob", [P, 2, 2, J], F32)
    pth, ptl = sb("pth", [P, JB, 2 * P], F32R), sb("ptl", [P, JB, 2 * P], F32R)
    p4_hi, p4 = sb("p4_hi", [4, 2 * P], F32R), sb("p4", [P, 2 * P], F32R)
    xb = sb("xb", [P, D], F32)
    bo_sb = sb("bo_sb", [P, D], F32)
    rows, stand = sb("rows", [4, 2], F32), sb("stand", [P, 1], F32)
    stats, mv, rstd = sb("stats", [P, G, 6], F32), sb("mv", [P, G, 2], F32), sb("rstd", [P, G], F32)
    maxes, sums = sb("maxes", [P, 2, 2], F32), sb("sums", [P, 2, 2], F32)
    neg_max, inv_sum = sb("neg_max", [P, 2, 2], F32), sb("inv_sum", [P, 2, 2], F32)
    assert sb.offset <= SBUF_END, sb.offset

    QK_BANKS = (2, 3, 0, 1, 2, 3)
    pt_ps = ps[:, 4, :]
    o_ps = ps[:, 5:7, :].rearrange("p a n -> p (a n)")[:, 0:KC * 2 * P]
    p4_ps = ps[0:4, 7, 0:2 * P]

    with semaphores(nc, "a_") as sem:
        x_in, const_in, mask_in = sem("x_in"), sem("const_in"), sem("mask_in")
        w_in = [sem(f"w_in{n}") for n in range(4)]
        w_hi, w_lo, zeroed = sem("w_hi"), sem("w_lo"), sem("zeroed")
        bn_done, mv_done, var_done, std_done, rstd_done = (sem(n) for n in ("bn_done", "mv_done", "var_done", "std_done", "rstd_done"))
        ctxT_in = [sem(f"ctxT_in{n}") for n in range(2)]
        ctx_in = [sem(f"ctx_in{n}") for n in range(2)]
        ctxT_hi, ctxT_lo, ctx_hi, ctx_lo, last_ready = (sem(n) for n in ("ctxT_hi", "ctxT_lo", "ctx_hi", "ctx_lo", "last_ready"))
        bias_ready = sem("bias_ready")
        xn_ready, xt_ps, xt_hi, xt_lo = (sem(n) for n in ("xn_ready", "xt_ps", "xt_hi", "xt_lo"))
        q_ps, q_hi, q_lo = sem("q_ps"), sem("q_hi"), sem("q_lo")
        qk_ps, qk_hi, qk_lo = sem("qk_ps"), sem("qk_hi"), sem("qk_lo")
        score_ps, max_ready, neg_ready, exp_ready = (sem(n) for n in ("score_ps", "max_ready", "neg_ready", "exp_ready"))
        inv_ready, prob_ready, pt_done, pt_hi, pt_lo, p4_hi_ready, p4_ready = (
            sem(n) for n in ("inv_ready", "prob_ready", "pt_done", "pt_hi", "pt_lo", "p4_hi_ready", "p4_ready"))
        pv_done, o_hi, o_lo = sem("pv_done"), sem("o_hi"), sem("o_lo")
        wv_done, ao_hi, ao_lo, wo_done, xb_ready, x_done = (sem(n) for n in ("wv_done", "ao_hi", "ao_lo", "wo_done", "xb_ready", "x_done"))

        def load_ctxT(sp, g, b):
            n = g * BPG + b
            if not (isinstance(g, int) and n < 2):
                sp.wait_ge(ctxT_lo, sp.snap(n - 1))
            sp.dma_start(ctxT_raw[:, b % 2], ctxT[bass.ds(n, 1)].rearrange("a (k p) j -> p (a k) j", p=P)).then_inc(ctxT_in[b % 2], 16)

        def load_ctx(sp, g, b):
            n = g * BPG + b
            if not (isinstance(g, int) and n < 2):
                sp.wait_ge(ctx_lo, sp.snap(n - 1))
                sp.wait_ge(last_ready, sp.snap(n - 1))
            sp.dma_start(ctx_raw[:, b % 2], ctx[bass.ds(n, 1), 0:JB * P].rearrange("a (k p) c -> p (a k) c", p=P)).then_inc(ctx_in[b % 2], 16)
            sp.dma_start(last_raw[:, b % 2, :], ctx[bass.ds(n, 1), J - 1].to_broadcast([4, CD])).then_inc(ctx_in[b % 2], 16)

        with nc.Block() as block:
            @block.sync
            def _(sp):
                sp.dma_start(x[:, :, :], x_dram.rearrange("(g p) d -> p g d", p=P)).then_inc(x_in, 16)
                sp.dma_start(ident[:, :], ident_dram).then_inc(const_in, 16)
                sp.dma_start(rows[:, :], rows_dram).then_inc(const_in, 16)
                sp.dma_start(bo_sb[:, :], bo.rearrange("(a n) -> a n", a=1).to_broadcast([P, D])).then_inc(const_in, 16)
                sp.dma_start(wq_raw[:, :, :], wq.rearrange("(k p) n -> p k n", p=P)).then_inc(w_in[0], 16)
                sp.dma_start(wk_raw[:, :, :], wkT.rearrange("(k p) n -> p k n", p=P)).then_inc(w_in[1], 16)
                load_ctxT(sp, 0, 0)
                sp.dma_start(mask_all[:, :], mask.rearrange("b j -> (b j)").rearrange("(a n) -> a n", a=1).to_broadcast([P, B * J])).then_inc(mask_in, 16)
                load_ctx(sp, 0, 0)
                load_ctxT(sp, 0, 1)
                sp.dma_start(wv_raw[:, :, :], wv.rearrange("(k p) n -> p k n", p=P)).then_inc(w_in[2], 16)
                sp.dma_start(wo_raw[:, :, :], wo.rearrange("(k p) n -> p k n", p=P)).then_inc(w_in[3], 16)
                load_ctxT(sp, 0, 2)
                load_ctx(sp, 0, 1)

                def group(g, last):
                    if not isinstance(g, int) or g:
                        load_ctx(sp, g, 1)
                    load_ctxT(sp, g, 3)
                    if not last:
                        load_ctxT(sp, g, 4)
                    load_ctx(sp, g, 2)
                    if not last:
                        load_ctxT(sp, g, 5)
                    load_ctx(sp, g, 3)
                    if not last:
                        load_ctx(sp, g, 4)
                        load_ctxT(sp, g, 6)

                group(0, False)
                with sp.Fori(1, G - 1) as g:
                    group(g, False)
                group(G - 1, True)

            @block.tensor
            def _(pe):
                def turn_tokens(g):
                    pe.wait_ge(xn_ready, g + 1)
                    for k in range(KD):
                        mm = pe.transpose(ps[:, 2, k * P:(k + 1) * P], xn[:, k * P:(k + 1) * P], ident[:, :])
                    mm.then_inc(xt_ps, 1)

                def queries(g):
                    pe.wait_ge(xt_lo, g + 1)
                    for m in range(XP):
                        for k in range(KD):
                            at = slice(m * P, (m + 1) * P)
                            mm = products(pe, ps[:, 0, at], (wqh[:, k, at], wql[:, k, at]), (xth[:, k, :], xtl[:, k, :]), k == 0, k == KD - 1)
                    mm.then_inc(q_ps, 1)

                def absorb(g, c):
                    pe.wait_ge(q_lo, g + 1)
                    if c == KC - 1:
                        pe.wait_ge(qk_lo, g * 2 * KC + 2)
                    for m in range(XP):
                        for s in range(2):
                            half = slice(s * DH, (s + 1) * DH)
                            mm = products(pe, ps[:, QK_BANKS[2 * c + s], m * P:(m + 1) * P],
                                          [t[half, m, c * P:(c + 1) * P] for t in (wkh, wkl)],
                                          [t[half, m, :] for t in (qh, ql)], True, True)
                    mm.then_inc(qk_ps, 1)

                def scores(g, b):
                    n = g * BPG + b
                    par = b % 2
                    pe.wait_ge(ctxT_lo, n + 1)
                    if b < 2:
                        pe.wait_ge(qk_lo, (g + 1) * 2 * KC)
                    else:
                        pe.wait_ge(max_ready, n - 1)
                    for s in range(2):
                        for c in range(KC):
                            w = [t[:, c, s, b].rearrange("p m i -> p (m i)") for t in (qkh, qkl)]
                            mm = products(pe, ps[:, 2 * par + s, 0:JE], w, (cTh[:, par, c, :], cTl[:, par, c, :]), c == 0, c == KC - 1)
                    mm.then_inc(score_ps, 1)

                def turn_probs(g, b):
                    n = g * BPG + b
                    pe.wait_ge(prob_ready, n + 1)
                    pe.wait_ge(p4_ready, n)
                    if b == 0:
                        pe.wait_ge(ao_lo, 2 * g)
                    for s in range(2):
                        for jb in range(JB):
                            pe.transpose(pt_ps[:, jb * 2 * P + s * P:jb * 2 * P + (s + 1) * P], prob[:, b % 2, s, jb * P:(jb + 1) * P], ident[:, :])
                        mm = pe.transpose(p4_ps[:, s * P:(s + 1) * P], prob[:, b % 2, s, J - 1:J].to_broadcast([P, 4]), ident[:, :])
                    mm.then_inc(pt_done, 1)

                def attend(g, b):
                    n = g * BPG + b
                    par = b % 2
                    pe.wait_ge(ctx_lo, n + 1)
                    pe.wait_ge(last_ready, n + 1)
                    pe.wait_ge(p4_ready, n + 1)
                    pe.wait_ge(o_lo, n)
                    if b == 0:
                        pe.wait_ge(x_done, g)
                    for c in range(KC):
                        at = slice(c * P, (c + 1) * P)
                        out = o_ps[:, c * 2 * P:(c + 1) * 2 * P]
                        for jb in range(JB):
                            products(pe, out, (ch[:, par, jb, at], cl[:, par, jb, at]), (pth[:, jb, :], ptl[:, jb, :]), jb == 0, False)
                        mm = pe.matmul(out, last4[:, par, at], p4[:, :], start=False, stop=True)
                    mm.then_inc(pv_done, 1)

                def values(g):
                    pe.wait_ge(o_lo, (g + 1) * BPG)
                    for m in range(XP):
                        for s in range(2):
                            at = slice((2 * m + s) * DH, (2 * m + s + 1) * DH)
                            for c in range(KC):
                                mm = products(pe, ps[0:DH, 4 if s else 7, m * P:(m + 1) * P],
                                              (wvh[:, c, at], wvl[:, c, at]),
                                              (oh[:, c, s * XP + m, :], ol[:, c, s * XP + m, :]), c == 0, c == KC - 1)
                    mm.then_inc(wv_done, 1)

                def project(g):
                    pe.wait_ge(ao_lo, 2 * g + 2)
                    for m in range(XP):
                        mm = products(pe, ps[:, 5, :], (aoh[:, m, :], aol[:, m, :]), (woh[:, m, :], wol[:, m, :]), m == 0, m == XP - 1)
                    mm.then_inc(wo_done, 1)

                def group(g, last):
                    turn_probs(g, 0)
                    scores(g, 2)
                    if not last:
                        turn_tokens(g + 1)
                    attend(g, 0)
                    turn_probs(g, 1)
                    if not last:
                        pe.wait_ge(xt_lo, g + 2)
                    scores(g, 3)
                    if not last:
                        pe.wait_ge(max_ready, g * BPG + 3)
                        queries(g + 1)
                    attend(g, 1)
                    turn_probs(g, 2)
                    if not last:
                        pe.wait_ge(max_ready, g * BPG + 4)
                        absorb(g + 1, 0)
                        absorb(g + 1, 1)
                    attend(g, 2)
                    turn_probs(g, 3)
                    if not last:
                        absorb(g + 1, 2)
                    attend(g, 3)
                    if not last:
                        scores(g + 1, 0)
                    values(g)
                    if not last:
                        scores(g + 1, 1)
                    project(g)

                pe.wait_ge(const_in, 48)
                pe.wait_ge(zeroed, 4)
                pe.wait_ge(w_lo, 4)
                turn_tokens(0)
                queries(0)
                for c in range(KC):
                    absorb(0, c)
                scores(0, 0)
                scores(0, 1)
                def step(g):
                    group(g, False)
                steps(pe, G - 1, step)
                group(G - 1, True)

            @block.scalar
            def _(act):
                def split_ctxT(g, b):
                    act.wait_ge(ctxT_in[b % 2], (g * (BPG // 2) + b // 2 + 1) * 16)
                    act.activation(cTh[:, b % 2, :, 0:J], ctxT_raw[:, b % 2], ACT.Copy).then_inc(ctxT_hi, 1)

                def split_ctx(g, b):
                    act.wait_ge(ctx_in[b % 2], (g * (BPG // 2) + b // 2 + 1) * 32)
                    act.activation(ch[:, b % 2, :, :], ctx_raw[:, b % 2], ACT.Copy).then_inc(ctx_hi, 1)
                    act.wait_ge(last_ready, g * BPG + b)
                    act.activation(last_hi[:, :], last_raw[:, b % 2, :], ACT.Copy).then_inc(ctx_hi, 1)

                def exponentials(g, b):
                    n = g * BPG + b
                    act.wait_ge(neg_ready, n + 1)
                    for s in range(2):
                        row = prob[:, b % 2, s, :]
                        mm = act.activation(row, row, ACT.Exp, bias=neg_max[:, b % 2, s:s + 1], accum_out=sums[:, b % 2, s:s + 1])
                    mm.then_inc(exp_ready, 1)

                def split_probs(g, b):
                    act.wait_ge(pt_done, g * BPG + b + 1)
                    act.activation(pth[:, :, :], pt_ps.rearrange("p (k n) -> p k n", k=JB), ACT.Copy).then_inc(pt_hi, 1)
                    act.activation(p4_hi[:, :], p4_ps, ACT.Copy).then_inc(p4_hi_ready, 1)

                def split_out(g, b):
                    act.wait_ge(pv_done, g * BPG + b + 1)
                    act.activation(oh[:, :, :, b * S:(b + 1) * S].rearrange("p c h n -> p (c h) n"),
                                   o_ps.rearrange("p (q n) -> p q n", n=S), ACT.Copy).then_inc(o_hi, 1)

                def split_tokens(g):
                    act.wait_ge(xt_ps, g + 1)
                    act.activation(xth[:, :, :], ps[:, 2, :].rearrange("p (k n) -> p k n", k=KD), ACT.Copy).then_inc(xt_hi, 1)

                def split_queries(g):
                    act.wait_ge(q_ps, g + 1)
                    act.activation(qh[:, :, :], ps[:, 0, :].rearrange("p (k n) -> p k n", k=XP), ACT.Copy, scale=DH ** -0.5).then_inc(q_hi, 1)

                def split_absorbed(g, c):
                    act.wait_ge(qk_ps, g * KC + c + 1)
                    for s in range(2):
                        act.activation(qkh[:, c, s].rearrange("p b m i -> p m b i"),
                                       ps[:, QK_BANKS[2 * c + s], :].rearrange("p (m b i) -> p m b i", m=XP, b=BPG), ACT.Copy).then_inc(qk_hi, 1)

                def group(g, last):
                    split_probs(g, 0)
                    split_ctx(g, 1)
                    split_ctxT(g, 3)
                    exponentials(g, 2)
                    if not last:
                        split_tokens(g + 1)
                        split_ctxT(g, 4)
                    split_out(g, 0)
                    split_probs(g, 1)
                    split_ctx(g, 2)
                    exponentials(g, 3)
                    if not last:
                        split_queries(g + 1)
                        split_ctxT(g, 5)
                    split_out(g, 1)
                    split_probs(g, 2)
                    if not last:
                        split_absorbed(g + 1, 0)
                        split_absorbed(g + 1, 1)
                    split_ctx(g, 3)
                    split_out(g, 2)
                    split_probs(g, 3)
                    if not last:
                        split_absorbed(g + 1, 2)
                        split_ctx(g, 4)
                    split_out(g, 3)
                    if not last:
                        exponentials(g, 4)
                        split_ctxT(g, 6)
                    act.wait_ge(wv_done, g + 1)
                    for s in range(2):
                        act.activation(aoh[s * DH:(s + 1) * DH, :, :], ps[0:DH, 4 if s else 7, :].rearrange("p (m n) -> p m n", m=XP), ACT.Copy).then_inc(ao_hi, 1)
                    if not last:
                        exponentials(g, 5)

                act.wait_ge(var_done, 1)
                act.activation(rstd[:, :], rstd[:, :], ACT.Sqrt).then_inc(std_done, 1)
                for n, (hi, w) in enumerate(((wqh, wq_raw), (wkh, wk_raw), (wvh, wv_raw), (woh, wo_raw))):
                    act.wait_ge(w_in[n], 16)
                    act.activation(hi[:, :, :], w[:, :, :], ACT.Copy).then_inc(w_hi, 1)
                split_tokens(0)
                split_queries(0)
                split_ctxT(0, 0)
                split_ctxT(0, 1)
                for c in range(KC):
                    split_absorbed(0, c)
                split_ctx(0, 0)
                exponentials(0, 0)
                split_ctxT(0, 2)
                exponentials(0, 1)
                with act.Fori(0, G - 1) as g:
                    group(g, False)
                group(G - 1, True)

            @block.vector
            def _(dve):
                def last_row(g, b):
                    n = g * BPG + b
                    dve.wait_ge(ctx_hi, 2 * n + 2)
                    dve.scalar_tensor_tensor(last4[0:4, b % 2, :], last_hi[:, :].bitcast(F32), rows[:, 0:1], last_raw[:, b % 2, :], ALU.mult, ALU.add).then_inc(last_ready, 1)

                def masked_max(g, b):
                    n = g * BPG + b
                    par = b % 2
                    dve.wait_ge(max_ready, n)
                    dve.tensor_scalar(mask_bias[:, :], mask_all[:, bass.ds(n * J, J)], FLT_MAX, -FLT_MAX, ALU.mult, ALU.add).then_inc(bias_ready, 1)
                    dve.wait_ge(score_ps, n + 1)
                    dve.wait_ge(bias_ready, n + 1)
                    if not (isinstance(g, int) and n < 2):
                        dve.wait_ge(pt_done, n - 1)
                    dve.memset(stand[:, :], 0.0)
                    for s in range(2):
                        mm = dve.tensor_tensor_reduce(prob[:, par, s, :], ps[:, 2 * par + s, 0:J], mask_bias[:, :], 1.0, -FLT_MAX,
                                                      ALU.add, ALU.max, maxes[:, par, s:s + 1])
                    mm.then_inc(max_ready, 1)
                    dve.wait_ge(max_ready, n + 1)
                    dve.tensor_scalar(neg_max[:, par, :], maxes[:, par, :], -1.0, None, ALU.mult).then_inc(neg_ready, 1)

                def normalise(g, b):
                    n = g * BPG + b
                    par = b % 2
                    dve.wait_ge(exp_ready, n + 1)
                    dve.reciprocal(inv_sum[:, par, :], sums[:, par, :]).then_inc(inv_ready, 1)
                    dve.wait_ge(inv_ready, n + 1)
                    for s in range(2):
                        row = prob[:, par, s, :]
                        mm = dve.tensor_scalar(row, row, inv_sum[:, par, s:s + 1], None, ALU.mult)
                    mm.then_inc(prob_ready, 1)

                dve.memset(cTh[:, :, :, J:JE].bitcast(F32), 0.0).then_inc(zeroed, 1)
                dve.memset(cTl[:, :, :, J:JE].bitcast(F32), 0.0).then_inc(zeroed, 1)
                dve.memset(last4[:, :, :].bitcast(F32), 0.0).then_inc(zeroed, 1)
                dve.memset(p4[:, :].bitcast(F32), 0.0).then_inc(zeroed, 1)
                dve.wait_ge(x_in, 16)
                for g in range(G):
                    dve.bn_stats(stats[:, g, :], x[:, g, :]).then_inc(bn_done, 1)
                dve.wait_ge(bn_done, G)
                for g in range(G):
                    dve.bn_aggr(mv[:, g, :], stats[:, g, :]).then_inc(mv_done, 1)
                dve.wait_ge(mv_done, G)
                dve.tensor_scalar(rstd[:, :], mv[:, :, 1], EPS, None, ALU.add).then_inc(var_done, 1)
                dve.wait_ge(std_done, 1)
                dve.reciprocal(rstd[:, :], rstd[:, :]).then_inc(rstd_done, 1)
                dve.wait_ge(const_in, 48)
                dve.wait_ge(zeroed, 4)
                dve.wait_ge(rstd_done, 1)

                def center(g):
                    at = slice(g, g + 1) if isinstance(g, int) else bass.ds(g, 1)
                    dve.wait_ge(xt_ps, g)
                    xg = x[:, at, :].rearrange("p a n -> p (a n)")
                    dve.tensor_scalar(xn[:, :], xg, mv[:, at, 0], rstd[:, at], ALU.subtract, ALU.mult).then_inc(xn_ready, 1)

                def split_tokens(g):
                    dve.wait_ge(xt_hi, g + 1)
                    dve.tensor_tensor(xtl[:, :, :], ps[:, 2, :].rearrange("p (k n) -> p k n", k=KD), xth[:, :, :].bitcast(F32), ALU.subtract).then_inc(xt_lo, 1)

                def split_queries(g):
                    dve.wait_ge(q_hi, g + 1)
                    dve.scalar_tensor_tensor(ql[:, :, :], ps[:, 0, :].rearrange("p (k n) -> p k n", k=XP), DH ** -0.5, qh[:, :, :].bitcast(F32), ALU.mult, ALU.subtract).then_inc(q_lo, 1)

                def split_absorbed(g, c):
                    for s in range(2):
                        dve.wait_ge(qk_hi, g * 2 * KC + 2 * c + s + 1)
                        dve.tensor_tensor(qkl[:, c, s].rearrange("p b m i -> p m b i"), ps[:, QK_BANKS[2 * c + s], :].rearrange("p (m b i) -> p m b i", m=XP, b=BPG),
                                          qkh[:, c, s].rearrange("p b m i -> p m b i").bitcast(F32), ALU.subtract).then_inc(qk_lo, 1)

                def split_probs(g, b):
                    dve.wait_ge(pt_hi, g * BPG + b + 1)
                    dve.tensor_tensor(ptl[:, :, :], pt_ps.rearrange("p (k n) -> p k n", k=JB), pth[:, :, :].bitcast(F32), ALU.subtract).then_inc(pt_lo, 1)
                    dve.wait_ge(p4_hi_ready, g * BPG + b + 1)
                    dve.scalar_tensor_tensor(p4[0:4, :], p4_hi[:, :].bitcast(F32), rows[:, 1:2], p4_ps, ALU.mult, ALU.add).then_inc(p4_ready, 1)

                def split_out(g, b):
                    dve.wait_ge(o_hi, g * BPG + b + 1)
                    at = slice(b * S, (b + 1) * S)
                    dve.tensor_tensor(ol[:, :, :, at].rearrange("p c h n -> p (c h) n"), o_ps.rearrange("p (q n) -> p q n", n=S),
                                      oh[:, :, :, at].rearrange("p c h n -> p (c h) n").bitcast(F32), ALU.subtract).then_inc(o_lo, 1)

                def group(g, last):
                    at = slice(g, g + 1) if isinstance(g, int) else bass.ds(g, 1)
                    xg = x[:, at, :].rearrange("p a n -> p (a n)")
                    dve.wait_ge(x_done, g)
                    dve.tensor_tensor(xb[:, :], xg, bo_sb[:, :], ALU.add).then_inc(xb_ready, 1)
                    split_probs(g, 0)
                    last_row(g, 1)
                    masked_max(g, 2)
                    if not last:
                        center(g + 1)
                    normalise(g, 2)
                    if not last:
                        split_tokens(g + 1)
                    split_out(g, 0)
                    split_probs(g, 1)
                    last_row(g, 2)
                    masked_max(g, 3)
                    normalise(g, 3)
                    if not last:
                        split_queries(g + 1)
                    split_out(g, 1)
                    split_probs(g, 2)
                    if not last:
                        split_absorbed(g + 1, 0)
                        split_absorbed(g + 1, 1)
                    last_row(g, 3)
                    split_out(g, 2)
                    split_probs(g, 3)
                    if not last:
                        split_absorbed(g + 1, 2)
                        last_row(g, 4)
                    split_out(g, 3)
                    if not last:
                        masked_max(g, 4)
                        normalise(g, 4)
                    for s in range(2):
                        dve.wait_ge(ao_hi, 2 * g + s + 1)
                        rows_ = slice(s * DH, (s + 1) * DH)
                        dve.tensor_tensor(aol[rows_, :, :], ps[0:DH, 4 if s else 7, :].rearrange("p (m n) -> p m n", m=XP), aoh[rows_, :, :].bitcast(F32), ALU.subtract).then_inc(ao_lo, 1)
                    if not last:
                        masked_max(g, 5)
                        normalise(g, 5)
                    dve.wait_ge(wo_done, g + 1)
                    dve.wait_ge(xb_ready, g + 1)
                    dve.tensor_tensor(xg, ps[:, 5, :], xb[:, :], ALU.add).then_inc(x_done, 1)

                center(0)
                for n, (hi, lo, w) in enumerate(((wqh, wql, wq_raw), (wkh, wkl, wk_raw), (wvh, wvl, wv_raw), (woh, wol, wo_raw))):
                    dve.wait_ge(w_hi, n + 1)
                    dve.tensor_tensor(lo[:, :, :], w[:, :, :], hi[:, :, :].bitcast(F32), ALU.subtract).then_inc(w_lo, 1)
                split_tokens(0)
                split_queries(0)
                for c in range(KC):
                    split_absorbed(0, c)
                last_row(0, 0)
                dve.wait_ge(mask_in, 16)
                masked_max(0, 0)
                normalise(0, 0)
                masked_max(0, 1)
                normalise(0, 1)
                def step(g):
                    group(g, False)
                steps(dve, G - 1, step)
                group(G - 1, True)

            @block.gpsimd
            def _(pool):
                def split_ctxT(g, b):
                    n = g * BPG + b
                    pool.wait_ge(ctxT_hi, n + 1)
                    pool.tensor_tensor(cTl[:, b % 2, :, 0:J], ctxT_raw[:, b % 2], cTh[:, b % 2, :, 0:J].bitcast(F32), ALU.subtract).then_inc(ctxT_lo, 1)

                def split_ctx(g, b):
                    pool.wait_ge(ctx_hi, 2 * (g * BPG + b) + 1)
                    pool.tensor_tensor(cl[:, b % 2, :, :], ctx_raw[:, b % 2], ch[:, b % 2, :, :].bitcast(F32), ALU.subtract).then_inc(ctx_lo, 1)

                def group(g, last):
                    split_ctx(g, 1)
                    split_ctxT(g, 3)
                    if not last:
                        split_ctxT(g, 4)
                    split_ctx(g, 2)
                    if not last:
                        split_ctxT(g, 5)
                    split_ctx(g, 3)
                    if not last:
                        split_ctx(g, 4)
                        split_ctxT(g, 6)

                split_ctxT(0, 0)
                split_ctxT(0, 1)
                split_ctx(0, 0)
                split_ctxT(0, 2)
                with pool.Fori(0, G - 1) as g:
                    group(g, False)
                group(G - 1, True)


def self_attention(nc, ps, wq, wk, wv, wo, rel_bias, onehot_dram, x, ident, xth, xtl, free):
    sb = Map(nc, free)
    xn = sb("b_xn", [P, 2, D], F32)
    wqk_raw, wv_raw, wo_raw = sb("b_wqk_raw", [P, 2, KD, P], F32), sb("b_wv_raw", [P, KD, P], F32), sb("b_wo_raw", [P, D], F32)
    wqkh, wqkl = sb("b_wqkh", [P, 2, KD, P], F32R), sb("b_wqkl", [P, 2, KD, P], F32R)
    wvh, wvl = sb("b_wvh", [P, KD, P], F32R), sb("b_wvl", [P, KD, P], F32R)
    woh, wol = sb("b_woh", [P, NP, D], F32R), sb("b_wol", [P, NP, D], F32R)
    qkh, qkl = sb("b_qkh", [P, 2, T], F32R), sb("b_qkl", [P, 2, T], F32R)
    vh, vl = sb("b_vh", [P, G, P], F32R), sb("b_vl", [P, G, P], F32R)
    prob = sb("b_prob", [P, 2, G, S], F32)
    block_prob = sb("b_block_prob", [P, 2, G, P], F32)
    ao = sb("b_ao", [P, NP, T], F32)
    bias = sb("b_bias", [P, SH, S], F32)
    maxes, sums = sb("b_maxes", [P, 2, G], F32), sb("b_sums", [P, 2, G], F32)
    stats, mv, rstd = sb("b_stats", [P, G, 6], F32), sb("b_mv", [P, G, 2], F32), sb("b_rstd", [P, G], F32)
    rel = sb("b_rel", [NBUCKET, SH], F32)
    onehot = nc.alloc_sbuf_tensor_at("b_onehot", [NBUCKET, S * P], F32, offset=sb.offset)
    pth, ptl = sb("b_pth", [P, 2, G, P], F32R), sb("b_ptl", [P, 2, G, P], F32R)
    final = Map(nc, sb.offset - 2 * G * P * 8)
    aoh, aol = final("b_aoh", [P, 2, NP, P], F32R), final("b_aol", [P, 2, NP, P], F32R)
    assert sb.offset <= SBUF_END, sb.offset

    units = ps[:, 0:4, :].rearrange("p a n -> p (a n)").rearrange("p (s g n) -> p s g n", s=2, g=G)

    with semaphores(nc, "b_") as sem:
        rel_in, bias_ps, bias_ready, zeroed = sem("rel_in"), sem("bias_ps"), sem("bias_ready"), sem("zeroed")
        bn_done, mv_done, var_done, std_done, rstd_done = (sem(n) for n in ("bn_done", "mv_done", "var_done", "std_done", "rstd_done"))
        xn_ready, xt_ps, xt_hi, xt_lo = (sem(n) for n in ("xn_ready", "xt_ps", "xt_hi", "xt_lo"))
        wqk_in, wv_in, wo_in = sem("wqk_in"), sem("wv_in"), sem("wo_in")
        wqk_hi, wqk_lo, wv_hi, wv_lo, wo_hi, wo_lo = (sem(n) for n in ("wqk_hi", "wqk_lo", "wv_hi", "wv_lo", "wo_hi", "wo_lo"))
        score_ps, score_read, max_done, shifted, exp_done = (sem(n) for n in ("score_ps", "score_read", "max_done", "shifted", "exp_done"))
        sum_done, inv_done, prob_ready = sem("sum_done"), sem("inv_done"), sem("prob_ready")
        v_ps, v_hi, v_lo, q_ps, k_ps, qk_hi, qk_lo = (sem(n) for n in ("v_ps", "v_hi", "v_lo", "q_ps", "k_ps", "qk_hi", "qk_lo"))
        pt_ps, pt_hi, pt_lo, pv_ps, ao_even, ao_odd = (sem(n) for n in ("pt_ps", "pt_hi", "pt_lo", "pv_ps", "ao_even", "ao_odd"))
        fin_hi, fin_lo, proj_ps, x_done = (sem(n) for n in ("fin_hi", "fin_lo", "proj_ps", "x_done"))

        with nc.Block() as block:
            @block.sync
            def _(sp):
                def load_wqk(p):
                    sp.wait_ge(wqk_lo, p)
                    at = bass.ds(p % NP * P, P) if isinstance(p, int) else bass.ds(sp.snap(p % NP * P), P)
                    sp.dma_start(wqk_raw[:, 0], wq[:, at].rearrange("(k p) n -> p k n", p=P)).then_inc(wqk_in, 16)
                    sp.dma_start(wqk_raw[:, 1], wk[:, at].rearrange("(k p) n -> p k n", p=P)).then_inc(wqk_in, 16)

                def load_wv(p):
                    sp.wait_ge(wv_lo, p)
                    sp.dma_start(wv_raw[:, :, :], wv[:, bass.ds(p % NP * P, P) if isinstance(p, int) else bass.ds(sp.snap(p % NP * P), P)].rearrange("(k p) n -> p k n", p=P)).then_inc(wv_in, 16)

                sp.dma_start(rel[:, :], rel_bias).then_inc(rel_in, 16)
                sp.dma_start(onehot[:, :], onehot_dram).then_inc(rel_in, 16)
                load_wqk(0)
                load_wv(0)
                load_wqk(1)
                def step(p):
                    two_on, one_on, here = (sp.snap(p + n) for n in (2, 1, 0)) if not isinstance(p, int) else (2, 1, 0)
                    load_wqk(two_on)
                    load_wv(one_on)
                    sp.wait_ge(wo_lo, here)
                    sp.dma_start(wo_raw[:, :], wo[bass.ds(p * P, P) if isinstance(p, int) else bass.ds(sp.snap(p * P), P), :]).then_inc(wo_in, 16)
                steps(sp, NP, step)

            @block.tensor
            def _(pe):
                def projected(p, a, half):
                    for k in range(KD):
                        at = slice(half * 512, (half + 1) * 512)
                        mm = products(pe, ps[:, (6, 4)[a] + half, :], (wqkh[:, a, k, :], wqkl[:, a, k, :]), (xth[:, k, at], xtl[:, k, at]), k == 0, k == KD - 1)
                    mm.then_inc((q_ps, k_ps)[a], 1)

                def pair(p, last):
                    pe.wait_ge(qk_lo, 4 * p + 4)
                    pe.wait_ge(pt_lo, 4 * p)
                    for g in range(G):
                        for s in range(2):
                            half, at = slice(s * DH, (s + 1) * DH), slice(g * P, (g + 1) * P)
                            mm = products(pe, units[:, s, g, :], [t[half, 0, at] for t in (qkh, qkl)], [t[half, 1, at] for t in (qkh, qkl)], True, True)
                    mm.then_inc(score_ps, 1)
                    pe.wait_ge(wv_lo, p + 1)
                    pe.wait_ge(ao_even, p)
                    for g in range(G):
                        for k in range(KD):
                            at = slice(g * P, (g + 1) * P)
                            mm = products(pe, ps[:, 4 + g // 4, g % 4 * P:(g % 4 + 1) * P], (xth[:, k, at], xtl[:, k, at]), (wvh[:, k, :], wvl[:, k, :]), k == 0, k == KD - 1)
                        if g % 4 == 3:
                            mm.then_inc(v_ps, 1)
                    if not last:
                        pe.wait_ge(wqk_lo, p + 2)
                        pe.wait_ge(ao_odd, p)
                        projected(p + 1, 0, 0)
                        projected(p + 1, 0, 1)
                    pe.wait_ge(prob_ready, p + 1)
                    for s in range(2):
                        for g in range(G):
                            mm = pe.transpose(units[:, s, g, :], block_prob[:, s, g, :], ident[:, :])
                            if g % 4 == 3:
                                mm.then_inc(pt_ps, 1)
                    if not last:
                        pe.wait_ge(v_lo, 2 * p + 2)
                        projected(p + 1, 1, 0)
                        projected(p + 1, 1, 1)
                    pe.wait_ge(pt_lo, 4 * p + 4)
                    if last:
                        pe.wait_ge(v_lo, 2 * p + 2)
                    for s in (1, 0):
                        if not last:
                            pe.wait_ge(qk_lo, 4 * p + (6 if s else 8))
                        elif s:
                            pe.wait_ge(ao_odd, p)
                        for g in range(G):
                            mm = products(pe, ps[0:DH, (4, 6)[s] + g // 4, g % 4 * P:(g % 4 + 1) * P],
                                          [t[:, g, s * DH:(s + 1) * DH] for t in (vh, vl)], (pth[:, s, g, :], ptl[:, s, g, :]), True, True)
                        mm.then_inc(pv_ps, 1)

                pe.wait_ge(rel_in, 32)
                for j in range(S):
                    mm = pe.matmul(ps[:, 7, j * SH:(j + 1) * SH], onehot[:, j * P:(j + 1) * P], rel[:, :], start=True, stop=True)
                mm.then_inc(bias_ps, 1)
                def step(gg):
                    for h in range(2):
                        g = gg * 2 + h
                        pe.wait_ge(xn_ready, g + 1)
                        pe.wait_ge(xt_lo, gg * 2)
                        for k in range(KD):
                            mm = pe.transpose(ps[:, h, k * P:(k + 1) * P], xn[:, h, k * P:(k + 1) * P], ident[:, :])
                        mm.then_inc(xt_ps, 1)
                steps(pe, G // 2, step)
                pe.wait_ge(wqk_lo, 1)
                pe.wait_ge(bias_ready, 1)
                for half in range(2):
                    pe.wait_ge(xt_lo, 4 * half + 4)
                    projected(0, 0, half)
                    projected(0, 1, half)
                def step(p):
                    pair(p, False)
                steps(pe, NP - 1, step)
                pair(NP - 1, True)
                pe.wait_ge(wo_lo, NP)
                def step(gg):
                    for h in range(2):
                        g = gg * 2 + h
                        pe.wait_ge(fin_lo, g + 1)
                        pe.wait_ge(x_done, gg * 2)
                        for k in range(NP):
                            mm = products(pe, ps[:, h, :], (aoh[:, h, k, :], aol[:, h, k, :]), (woh[:, k, :], wol[:, k, :]), k == 0, k == NP - 1)
                        mm.then_inc(proj_ps, 1)
                steps(pe, G // 2, step)

            @block.scalar
            def _(act):
                def split_projected(p, a, half):
                    act.wait_ge((q_ps, k_ps)[a], 2 * p + half + 1)
                    act.activation(qkh[:, a, half * 512:(half + 1) * 512], ps[:, (6, 4)[a] + half, :], ACT.Copy).then_inc(qk_hi, 1)

                def split_values(p, n):
                    act.wait_ge(v_ps, 2 * p + n + 1)
                    act.activation(vh[:, 4 * n:4 * n + 4, :], ps[:, 4 + n, :].rearrange("p (g n) -> p g n", g=4), ACT.Copy).then_inc(v_hi, 1)

                def split_wqk(p):
                    act.wait_ge(wqk_in, (p + 1) * 32)
                    act.wait_ge(k_ps, 2 * p)
                    act.activation(wqkh[:, :, :, :], wqk_raw[:, :, :, :], ACT.Copy).then_inc(wqk_hi, 1)

                def split_wv(p):
                    act.wait_ge(wv_in, (p + 1) * 16)
                    act.wait_ge(v_ps, 2 * p)
                    act.activation(wvh[:, :, :], wv_raw[:, :, :], ACT.Copy).then_inc(wv_hi, 1)

                def pair(p, last):
                    split_values(p, 0)
                    act.wait_ge(shifted, p + 1)
                    act.activation(prob[:, :, :, :], prob[:, :, :, :], ACT.Exp).then_inc(exp_done, 1)
                    split_values(p, 1)
                    if not last:
                        split_projected(p + 1, 0, 0)
                        split_projected(p + 1, 0, 1)
                    for n in range(4):
                        act.wait_ge(pt_ps, 4 * p + n + 1)
                        act.activation(pth[:, n // 2, n % 2 * 4:n % 2 * 4 + 4, :], units[:, n // 2, n % 2 * 4:n % 2 * 4 + 4, :], ACT.Copy).then_inc(pt_hi, 1)
                    if not last:
                        split_projected(p + 1, 1, 0)
                        split_projected(p + 1, 1, 1)
                    at = slice(p, p + 1) if last else bass.ds(p, 1)
                    act.wait_ge(wo_in, (p + 1) * 16)
                    act.activation(woh[:, at, :].rearrange("p a n -> p (a n)"), wo_raw[:, :], ACT.Copy).then_inc(wo_hi, 1)
                    act.wait_ge(pv_ps, 2 * p + 1)
                    act.activation(ao[DH:P, at, :].rearrange("p a n -> p (a n)"), ps[0:DH, 6:8, :].rearrange("p a n -> p (a n)"), ACT.Copy).then_inc(ao_odd, 1)
                    if not last:
                        split_wv(p + 1)
                        split_wqk(p + 2)

                act.wait_ge(var_done, 1)
                act.activation(rstd[:, :], rstd[:, :], ACT.Sqrt).then_inc(std_done, 1)
                act.wait_ge(bias_ps, 1)
                act.activation(bias[:, :, :].rearrange("p h j -> p j h"), ps[:, 7, :].rearrange("p (j h) -> p j h", h=SH), ACT.Copy).then_inc(bias_ready, 1)
                split_wqk(0)
                split_wv(0)
                with act.Fori(0, G // 2) as gg:
                    for h in range(2):
                        g = gg * 2 + h
                        act.wait_ge(xt_ps, g + 1)
                        act.activation(xth[:, :, bass.ds(g * P, P)], ps[:, h, :].rearrange("p (k n) -> p k n", k=KD), ACT.Copy).then_inc(xt_hi, 1)
                for half in range(2):
                    for a in range(2):
                        split_projected(0, a, half)
                split_wqk(1)
                with act.Fori(0, NP - 1) as p:
                    pair(p, False)
                pair(NP - 1, True)
                def step(gg):
                    for h in range(2):
                        g = gg * 2 + h
                        act.wait_ge(ao_even, NP)
                        act.wait_ge(ao_odd, NP)
                        act.wait_ge(proj_ps, gg * 2)
                        act.activation(aoh[:, h], ao[:, :, bass.ds(g * P, P)], ACT.Copy).then_inc(fin_hi, 1)
                steps(act, G // 2, step)

            @block.vector
            def _(dve):
                def split_projected(p, a, half, n):
                    dve.wait_ge(qk_hi, 4 * p + n + 1)
                    at = slice(half * 512, (half + 1) * 512)
                    dve.tensor_tensor(qkl[:, a, at], ps[:, (6, 4)[a] + half, :], qkh[:, a, at].bitcast(F32), ALU.subtract).then_inc(qk_lo, 1)

                def split_values(p, n):
                    dve.wait_ge(v_hi, 2 * p + n + 1)
                    at = slice(4 * n, 4 * n + 4)
                    dve.tensor_tensor(vl[:, at, :], ps[:, 4 + n, :].rearrange("p (g n) -> p g n", g=4), vh[:, at, :].bitcast(F32), ALU.subtract).then_inc(v_lo, 1)

                def pair(p, last):
                    heads = slice(2 * p, 2 * p + 2) if last else bass.ds(p * 2, 2)
                    dve.wait_ge(score_ps, p + 1)
                    dve.wait_ge(prob_ready, p)
                    for r in range(BPG):
                        at = slice(r * S, (r + 1) * S)
                        shared = bias[at, heads, :].rearrange("p h (a j) -> p h a j", a=1).to_broadcast([S, 2, G, S])
                        mm = dve.tensor_tensor(prob[at], units[at, :, :, at], shared, ALU.add)
                    mm.then_inc(score_read, 1)
                    dve.wait_ge(score_read, p + 1)
                    dve.tensor_reduce(maxes[:, :, :], prob[:, :, :, :], AX_X, ALU.max).then_inc(max_done, 1)
                    dve.wait_ge(max_done, p + 1)
                    dve.tensor_tensor(prob[:, :, :, :], prob[:, :, :, :], maxes[:, :, :].rearrange("p s (g a) -> p s g a", a=1).to_broadcast([P, 2, G, S]), ALU.subtract).then_inc(shifted, 1)
                    split_values(p, 0)
                    dve.wait_ge(exp_done, p + 1)
                    dve.tensor_reduce(sums[:, :, :], prob[:, :, :, :], AX_X, ALU.add).then_inc(sum_done, 1)
                    dve.wait_ge(sum_done, p + 1)
                    dve.reciprocal(sums[:, :, :], sums[:, :, :]).then_inc(inv_done, 1)
                    dve.wait_ge(inv_done, p + 1)
                    dve.wait_ge(pt_ps, 4 * p)
                    for r in range(BPG):
                        at = slice(r * S, (r + 1) * S)
                        mm = dve.tensor_tensor(block_prob[at, :, :, at], prob[at], sums[at].rearrange("p s (g a) -> p s g a", a=1).to_broadcast([S, 2, G, S]), ALU.mult)
                    mm.then_inc(prob_ready, 1)
                    split_values(p, 1)
                    if not last:
                        split_projected(p + 1, 0, 0, 0)
                        split_projected(p + 1, 0, 1, 1)
                    for n in range(4):
                        dve.wait_ge(pt_hi, 4 * p + n + 1)
                        at = slice(n % 2 * 4, n % 2 * 4 + 4)
                        dve.tensor_tensor(ptl[:, n // 2, at, :], units[:, n // 2, at, :], pth[:, n // 2, at, :].bitcast(F32), ALU.subtract).then_inc(pt_lo, 1)
                    if not last:
                        split_projected(p + 1, 1, 0, 2)
                        split_projected(p + 1, 1, 1, 3)
                    at = slice(p, p + 1) if last else bass.ds(p, 1)
                    dve.wait_ge(pv_ps, 2 * p + 2)
                    dve.tensor_copy(ao[0:DH, at, :].rearrange("p a n -> p (a n)"), ps[0:DH, 4:6, :].rearrange("p a n -> p (a n)")).then_inc(ao_even, 1)

                for g in range(G):
                    dve.bn_stats(stats[:, g, :], x[:, g, :]).then_inc(bn_done, 1)
                dve.wait_ge(bn_done, G)
                for g in range(G):
                    dve.bn_aggr(mv[:, g, :], stats[:, g, :]).then_inc(mv_done, 1)
                dve.wait_ge(mv_done, G)
                dve.tensor_scalar(rstd[:, :], mv[:, :, 1], EPS, None, ALU.add).then_inc(var_done, 1)
                dve.memset(block_prob[:, :, :, :], 0.0).then_inc(zeroed, 1)
                dve.wait_ge(std_done, 1)
                dve.reciprocal(rstd[:, :], rstd[:, :]).then_inc(rstd_done, 1)
                dve.wait_ge(rstd_done, 1)

                def center(gg, h):
                    g = gg * 2 + h
                    at = slice(g, g + 1) if isinstance(g, int) else bass.ds(g, 1)
                    dve.tensor_scalar(xn[:, h, :], x[:, at, :].rearrange("p a n -> p (a n)"), mv[:, at, 0], rstd[:, at], ALU.subtract, ALU.mult).then_inc(xn_ready, 1)

                def turned(gg, h):
                    g = gg * 2 + h
                    dve.wait_ge(xt_hi, g + 1)
                    at = slice(g * P, g * P + P) if isinstance(g, int) else bass.ds(g * P, P)
                    dve.tensor_tensor(xtl[:, :, at], ps[:, h, :].rearrange("p (k n) -> p k n", k=KD), xth[:, :, at].bitcast(F32), ALU.subtract).then_inc(xt_lo, 1)

                center(0, 0)
                center(0, 1)
                with dve.Fori(0, G // 2 - 1) as gg:
                    for h in range(2):
                        turned(gg, h)
                        center(gg + 1, h)
                turned(G // 2 - 1, 0)
                turned(G // 2 - 1, 1)
                for half in range(2):
                    for a in range(2):
                        split_projected(0, a, half, 2 * half + a)
                dve.wait_ge(bias_ready, 1)
                dve.wait_ge(zeroed, 1)
                def step(p):
                    pair(p, False)
                steps(dve, NP - 1, step)
                pair(NP - 1, True)
                with dve.Fori(0, G // 2) as gg:
                    for h in range(2):
                        g = gg * 2 + h
                        dve.wait_ge(fin_hi, g + 1)
                        dve.tensor_tensor(aol[:, h], ao[:, :, bass.ds(g * P, P)], aoh[:, h].bitcast(F32), ALU.subtract).then_inc(fin_lo, 1)
                        dve.wait_ge(proj_ps, g + 1)
                        xg = x[:, bass.ds(g, 1), :].rearrange("p a n -> p (a n)")
                        dve.tensor_tensor(xg, xg, ps[:, h, :], ALU.add).then_inc(x_done, 1)

            @block.gpsimd
            def _(pool):
                def split_wqk(p):
                    pool.wait_ge(wqk_hi, p + 1)
                    pool.tensor_tensor(wqkl[:, :, :, :], wqk_raw[:, :, :, :], wqkh[:, :, :, :].bitcast(F32), ALU.subtract).then_inc(wqk_lo, 1)

                def split_wv(p):
                    pool.wait_ge(wv_hi, p + 1)
                    pool.tensor_tensor(wvl[:, :, :], wv_raw[:, :, :], wvh[:, :, :].bitcast(F32), ALU.subtract).then_inc(wv_lo, 1)

                split_wqk(0)
                split_wv(0)
                split_wqk(1)
                def pair(p, last):
                    at = slice(p, p + 1) if last else bass.ds(p, 1)
                    pool.wait_ge(wo_hi, p + 1)
                    pool.tensor_tensor(wol[:, at, :].rearrange("p a n -> p (a n)"), wo_raw[:, :], woh[:, at, :].rearrange("p a n -> p (a n)").bitcast(F32), ALU.subtract).then_inc(wo_lo, 1)
                    if not last:
                        split_wv(p + 1)
                        split_wqk(p + 2)
                with pool.Fori(0, NP - 1) as p:
                    pair(p, False)
                pair(NP - 1, True)


def mixture(nc, ps, gate, sg, su, sd, wg, wu, wd, xn_dram, out, x, ident, xth, xtl, free):
    sb = Map(nc, free)
    slots = sb("c_slots", [P, NI, 3, 4, 512], F32)
    EARLY = 2
    early = Map(nc, free + EARLY * 3 * 4 * 512 * 4)
    sdh, sdl = early("c_sdh", [P, KI, D], F32R), early("c_sdl", [P, KI, D], F32R)
    hsh, hsl = early("c_hsh", [P, 1, KI, P], F32R), early("c_hsl", [P, 1, KI, P], F32R)
    s_raw = early("c_s_raw", [P, 2, KD, P], F32)
    sd_raw = early("c_sd_raw", [P, D], F32)
    assert early.offset <= sb.offset
    hs = sb("c_hs", [P, KI, T], F32)
    sguh, sgul = sb("c_sguh", [P, 2, KD, P], F32R), sb("c_sgul", [P, 2, KD, P], F32R)
    xn = sb("c_xn", [P, 2, D], F32)
    gelu_s = sb("c_gelu_s", [P, 2, D], F32)
    y = sb("c_y", [P, 2, D], F32)
    stats, mv, rstd = sb("c_stats", [P, G, 6], F32), sb("c_mv", [P, G, 2], F32), sb("c_rstd", [P, G], F32)
    gate_raw, gateh, gatel = sb("c_gate_raw", [P, KD, E], F32), sb("c_gateh", [P, KD, E], F32R), sb("c_gatel", [P, KD, E], F32R)
    route, peak, total = sb("c_route", [P, G, E], F32), sb("c_peak", [P, G], F32), sb("c_total", [P, G], F32)
    score = sb("c_score", [E, T], F32)
    best8, best8_at = sb("c_best8", [E, 8], F32), sb("c_best8_at", [E, 8], U32)
    best, best_at = sb("c_best", [E, C], F32), sb("c_best_at", [E, C], F32)
    weight, token = sb("c_weight", [C, E], F32), sb("c_token", [C, E], U32)
    ex = Map(nc, free + NI * 3 * 4 * 512 * 4)
    xg, xgt = ex("c_xg", [C, D], F32), ex("c_xgt", [P, KD, C], F32)
    gelu_e, h, ht = ex("c_gelu_e", [C, 2, D], F32), ex("c_h", [C, 2, D], F32), ex("c_ht", [P, 2, 4, C], F32)
    assert ex.offset <= free + NI * 3 * 4 * 512 * 4 + KI * T * 4
    eo = sb("c_eo", [C, D], F32)
    gather_at, scatter_at = sb("c_gather_at", [C, 1], U32), sb("c_scatter_at", [C, 1], U32)
    stand, pool_stand = sb("c_stand", [P, 1], F32), sb("c_pool_stand", [P, 1], F32)
    assert sb.offset <= SBUF_END, sb.offset

    with semaphores(nc, "c_") as sem:
        gate_in, s_in, sd_in = sem("gate_in"), sem("s_in"), sem("sd_in")
        slot_in = [[sem(f"slot_in{n}_{a}") for a in range(3)] for n in range(NI)]
        bn_done, mv_done, var_done, std_done, rstd_done = (sem(n) for n in ("bn_done", "mv_done", "var_done", "std_done", "rstd_done"))
        xn_ready, xt_ps, xt_hi, xt_lo = (sem(n) for n in ("xn_ready", "xt_ps", "xt_hi", "xt_lo"))
        xn_out = [sem(f"xn_out{n}") for n in range(2)]
        gate_hi, gate_lo, logit_ps, shifted, exp_done, sum_done, inv_done, route_ready = (
            sem(n) for n in ("gate_hi", "gate_lo", "logit_ps", "shifted", "exp_done", "sum_done", "inv_done", "route_ready"))
        peak_done, turn_ps, score_ready = sem("peak_done"), sem("turn_ps"), sem("score_ready")
        found, placed, removed, picked_ps, token_ready = (sem(n) for n in ("found", "placed", "removed", "picked_ps", "token_ready"))
        sgu_hi, sgu_lo, sd_hi, sd_lo = (sem(n) for n in ("sgu_hi", "sgu_lo", "sd_hi", "sd_lo"))
        sg_ps, su_ps, s_gelu, hs_ready = (sem(n) for n in ("sg_ps", "su_ps", "s_gelu", "hs_ready"))
        hs_hi, hs_lo, down_ps, y_ready = (sem(n) for n in ("hs_hi", "hs_lo", "down_ps", "y_ready"))
        y_out = [sem(f"y_out{n}") for n in range(2)]
        gather_idx, scatter_idx, gathered, scattered = (sem(n) for n in ("gather_idx", "scatter_idx", "gathered", "scattered"))
        xgt_ps, xgt_ready, g_ps, u_ps, e_gelu, h_ready, ht_ps, ht_ready, eo_ps, eo_ready = (
            sem(n) for n in ("xgt_ps", "xgt_ready", "g_ps", "u_ps", "e_gelu", "h_ready", "ht_ps", "ht_ready", "eo_ps", "eo_ready"))
        d_used = sem("d_used")

        with nc.Block() as block:
            @block.sync
            def _(sp):
                def load_shared(c):
                    sp.wait_ge(sgu_lo, c)
                    sp.dma_start(s_raw[:, 0], sg[bass.ds(c, 1)].rearrange("a p k n -> p (a k) n")).then_inc(s_in, 16)
                    sp.dma_start(s_raw[:, 1], su[bass.ds(c, 1)].rearrange("a p k n -> p (a k) n")).then_inc(s_in, 16)
                    sp.wait_ge(sd_lo, c)
                    sp.dma_start(sd_raw[:, :], sd[bass.ds(c * P, P), :]).then_inc(sd_in, 16)

                def load_slot(e, n, a):
                    w = (wg, wu, wd)[a]
                    sp.dma_start(slots[:, n, a], w[bass.ds(e, 1), n].rearrange("a p k n -> p (a k) n")).then_inc(slot_in[n][a], 16)

                sp.dma_start(gate_raw[:, :, :], gate.rearrange("(k p) n -> p k n", p=P)).then_inc(gate_in, 16)
                load_shared(0)
                for n in range(EARLY):
                    for a in range(3):
                        load_slot(0, n, a)
                with sp.Fori(0, G // 2) as gg:
                    counts = [sp.snap(gg * 2 + h + 1) for h in range(2)]
                    for h in range(2):
                        sp.wait_ge(xn_ready, counts[h])
                        sp.dma_start(xn_dram[bass.ds((gg * 2 + h) * P, P), :], xn[:, h, :]).then_inc(xn_out[h], 16)
                with sp.Fori(1, KI) as c:
                    load_shared(c)
                with sp.Fori(0, G // 2) as gg:
                    counts = [sp.snap(gg * 2 + h + 1) for h in range(2)]
                    for h in range(2):
                        sp.wait_ge(y_ready, counts[h])
                        sp.dma_start(out[bass.ds((gg * 2 + h) * P, P), :], y[:, h, :]).then_inc(y_out[h], 16)
                for n in range(EARLY, NI):
                    for a in range(3):
                        load_slot(0, n, a)
                with sp.Fori(1, E) as e:
                    used = [[sp.snap((e - 1) * NI + n + 1) for n in range(NI)]]
                    for n in range(NI):
                        for a, s in enumerate((g_ps, u_ps, d_used)):
                            sp.wait_ge(s, used[0][n])
                            load_slot(e, n, a)
                sp.wait_ge(scattered, 16 * E)

            @block.tensor
            def _(pe):
                def hidden(c):
                    pe.wait_ge(sgu_lo, c + 1)
                    for half in range(2):
                        at = slice(half * 512, (half + 1) * 512)
                        for a, s in ((0, sg_ps), (1, su_ps)):
                            for k in range(KD):
                                mm = products(pe, ps[:, 2 * half + a, :], (sguh[:, a, k, :], sgul[:, a, k, :]), (xth[:, k, at], xtl[:, k, at]), k == 0, k == KD - 1)
                            mm.then_inc(s, 1)

                def step(gg):
                    for h_ in range(2):
                        g = gg * 2 + h_
                        pe.wait_ge(xn_ready, g + 1)
                        pe.wait_ge(xt_lo, gg * 2)
                        for k in range(KD):
                            mm = pe.transpose(ps[:, h_, k * P:(k + 1) * P], xn[:, h_, k * P:(k + 1) * P], ident[:, :])
                        mm.then_inc(xt_ps, 1)
                steps(pe, G // 2, step)
                pe.wait_ge(gate_lo, 1)
                pe.wait_ge(xt_lo, G)
                for g in range(G):
                    for k in range(KD):
                        at = slice(g * P, (g + 1) * P)
                        mm = products(pe, ps[:, 7, g * E:(g + 1) * E], (xth[:, k, at], xtl[:, k, at]), (gateh[:, k, :], gatel[:, k, :]), k == 0, k == KD - 1)
                mm.then_inc(logit_ps, 1)
                hidden(0)
                pe.wait_ge(route_ready, 1)
                for g in range(G):
                    mm = pe.transpose(ps[0:E, 4 + g // 4, g % 4 * P:(g % 4 + 1) * P], route[:, g, :], ident[:, :])
                mm.then_inc(turn_ps, 1)
                with pe.Fori(1, KI) as c:
                    pe.wait_ge(hs_ready, c * 2)
                    hidden(c)
                pe.wait_ge(sd_lo, KI)
                def step(g):
                    pe.wait_ge(hs_lo, g + 1)
                    pe.wait_ge(y_ready, g)
                    for k in range(KI):
                        mm = products(pe, ps[:, 6, :], (hsh[:, 0, k, :], hsl[:, 0, k, :]), (sdh[:, k, :], sdl[:, k, :]), k == 0, k == KI - 1)
                    mm.then_inc(down_ps, 1)
                steps(pe, G, step)
                pe.wait_ge(removed, C // 8)
                pe.transpose(ps[:, 7, 0:E], best[:, :], ident[0:E, 0:E])
                pe.transpose(ps[:, 7, E:2 * E], best_at[:, :], ident[0:E, 0:E]).then_inc(picked_ps, 1)

                def turn_rows(e):
                    pe.wait_ge(gathered, (e + 1) * 16)
                    for k in range(KD):
                        mm = pe.transpose(ps[:, 6, k * P:(k + 1) * P], xg[:, k * P:(k + 1) * P], ident[:, :])
                    mm.then_inc(xgt_ps, 1)

                def gate_up(e, n):
                    for a, s in ((0, g_ps), (1, u_ps)):
                        pe.wait_ge(slot_in[n][a], (e + 1) * 16)
                        for k in range(KD):
                            mm = pe.matmul(ps[:, n % 2 * 2 + a, :], xgt[:, k, :], slots[:, n, a, k, :], start=(k == 0), stop=(k == KD - 1))
                        mm.then_inc(s, 1)

                def down(e, n):
                    pe.wait_ge(h_ready, e * NI + n + 1)
                    pe.wait_ge(ht_ready, e * NI + n)
                    for k in range(4):
                        mm = pe.transpose(ps[:, 4, k * P:(k + 1) * P], h[:, n % 2, k * P:(k + 1) * P], ident[:, :])
                    mm.then_inc(ht_ps, 1)
                    pe.wait_ge(ht_ready, e * NI + n + 1)
                    pe.wait_ge(slot_in[n][2], (e + 1) * 16)
                    if n == 0:
                        pe.wait_ge(eo_ready, e)
                    for k in range(4):
                        mm = pe.matmul(ps[:, 5, :], ht[:, n % 2, k, :], slots[:, n, 2, k, :], start=(n == 0 and k == 0), stop=(n == NI - 1 and k == 3))
                    mm.then_inc(d_used, 1)

                def expert(e, last):
                    gate_up(e, 1)
                    down(e, 0)
                    gate_up(e, 2)
                    down(e, 1)
                    gate_up(e, 3)
                    down(e, 2)
                    if not last:
                        turn_rows(e + 1)
                        pe.wait_ge(xgt_ready, e + 2)
                        gate_up(e + 1, 0)
                    down(e, 3)

                turn_rows(0)
                pe.wait_ge(xgt_ready, 1)
                gate_up(0, 0)
                def step(e):
                    expert(e, False)
                steps(pe, E - 1, step)
                expert(E - 1, True)

            @block.scalar
            def _(act):
                def split_shared(c):
                    at = slice(c, c + 1) if isinstance(c, int) else bass.ds(c, 1)
                    act.wait_ge(s_in, (c + 1) * 32)
                    act.wait_ge(su_ps, 2 * c)
                    act.activation(sguh[:, :, :, :], s_raw[:, :, :, :], ACT.Copy).then_inc(sgu_hi, 1)
                    act.wait_ge(sd_in, (c + 1) * 16)
                    act.activation(sdh[:, at, :].rearrange("p a n -> p (a n)"), sd_raw[:, :], ACT.Copy).then_inc(sd_hi, 1)

                def gelu_shared(c):
                    for half in range(2):
                        act.wait_ge(sg_ps, 2 * c + half + 1)
                        if not isinstance(c, int):
                            act.wait_ge(hs_ready, 2 * c + half - 1)
                        act.activation(gelu_s[:, half, :], ps[:, 2 * half, :], ACT.Gelu).then_inc(s_gelu, 1)

                act.wait_ge(var_done, 1)
                act.activation(rstd[:, :], rstd[:, :], ACT.Sqrt).then_inc(std_done, 1)
                act.wait_ge(gate_in, 16)
                act.activation(gateh[:, :, :], gate_raw[:, :, :], ACT.Copy).then_inc(gate_hi, 1)
                split_shared(0)
                with act.Fori(0, G // 2) as gg:
                    for h_ in range(2):
                        g = gg * 2 + h_
                        act.wait_ge(xt_ps, g + 1)
                        act.activation(xth[:, :, bass.ds(g * P, P)], ps[:, h_, :].rearrange("p (k n) -> p k n", k=KD), ACT.Copy).then_inc(xt_hi, 1)
                act.wait_ge(shifted, 1)
                act.activation(route[:, :, :], route[:, :, :], ACT.Exp).then_inc(exp_done, 1)
                gelu_shared(0)
                with act.Fori(1, KI) as c:
                    split_shared(c)
                    gelu_shared(c)
                def step(g):
                    act.wait_ge(hs_ready, 2 * KI)
                    act.wait_ge(down_ps, g)
                    act.activation(hsh[:, 0], hs[:, :, bass.ds(g * P, P)], ACT.Copy).then_inc(hs_hi, 1)
                steps(act, G, step)

                def gelu_expert(e, n):
                    act.wait_ge(g_ps, e * NI + n + 1)
                    if not (isinstance(e, int) and e == 0 and n < 2):
                        act.wait_ge(h_ready, e * NI + n - 1)
                    act.activation(gelu_e[:, n % 2, :], ps[:, n % 2 * 2, :], ACT.Gelu).then_inc(e_gelu, 1)

                def turned_rows(e):
                    act.wait_ge(xgt_ps, e + 1)
                    act.wait_ge(u_ps, e * NI)
                    act.activation(xgt[:, :, :], ps[:, 6, :].rearrange("p (k n) -> p k n", k=KD), ACT.Copy).then_inc(xgt_ready, 1)

                def expert(e, last):
                    for n in range(1, NI):
                        gelu_expert(e, n)
                    if not last:
                        turned_rows(e + 1)
                        gelu_expert(e + 1, 0)

                turned_rows(0)
                gelu_expert(0, 0)
                expert(0, False)
                with act.Fori(1, E - 1) as e:
                    expert(e, False)
                expert(E - 1, True)

            @block.vector
            def _(dve):
                for g in range(G):
                    dve.bn_stats(stats[:, g, :], x[:, g, :]).then_inc(bn_done, 1)
                dve.wait_ge(bn_done, G)
                for g in range(G):
                    dve.bn_aggr(mv[:, g, :], stats[:, g, :]).then_inc(mv_done, 1)
                dve.wait_ge(mv_done, G)
                dve.tensor_scalar(rstd[:, :], mv[:, :, 1], EPS, None, ALU.add).then_inc(var_done, 1)
                dve.wait_ge(std_done, 1)
                dve.reciprocal(rstd[:, :], rstd[:, :]).then_inc(rstd_done, 1)
                dve.wait_ge(rstd_done, 1)

                def center(gg, h_):
                    g = gg * 2 + h_
                    if not isinstance(gg, int):
                        dve.wait_ge(xn_out[h_], gg * 16)
                    at = slice(g, g + 1) if isinstance(g, int) else bass.ds(g, 1)
                    dve.tensor_scalar(xn[:, h_, :], x[:, at, :].rearrange("p a n -> p (a n)"), mv[:, at, 0], rstd[:, at], ALU.subtract, ALU.mult).then_inc(xn_ready, 1)

                def turned(gg, h_):
                    g = gg * 2 + h_
                    dve.wait_ge(xt_hi, g + 1)
                    at = slice(g * P, g * P + P) if isinstance(g, int) else bass.ds(g * P, P)
                    dve.tensor_tensor(xtl[:, :, at], ps[:, h_, :].rearrange("p (k n) -> p k n", k=KD), xth[:, :, at].bitcast(F32), ALU.subtract).then_inc(xt_lo, 1)

                center(0, 0)
                center(0, 1)
                with dve.Fori(0, G // 2 - 1) as gg:
                    for h_ in range(2):
                        turned(gg, h_)
                        center(gg + 1, h_)
                turned(G // 2 - 1, 0)
                turned(G // 2 - 1, 1)
                dve.wait_ge(logit_ps, 1)
                logits = ps[:, 7, 0:G * E].rearrange("p (g e) -> p g e", g=G)
                wide = lambda t: t[:, :].rearrange("p (g a) -> p g a", a=1).to_broadcast([P, G, E])
                dve.tensor_reduce(peak[:, :], logits, AX_X, ALU.max).then_inc(peak_done, 1)
                dve.wait_ge(peak_done, 1)
                dve.tensor_tensor(route[:, :, :], logits, wide(peak), ALU.subtract).then_inc(shifted, 1)
                dve.wait_ge(exp_done, 1)
                dve.tensor_reduce(total[:, :], route[:, :, :], AX_X, ALU.add).then_inc(sum_done, 1)
                dve.wait_ge(sum_done, 1)
                dve.reciprocal(total[:, :], total[:, :]).then_inc(inv_done, 1)
                dve.wait_ge(inv_done, 1)
                dve.tensor_tensor(route[:, :, :], route[:, :, :], wide(total), ALU.mult).then_inc(route_ready, 1)

                def gated(c, half):
                    dve.wait_ge(s_gelu, 2 * c + half + 1)
                    dve.wait_ge(su_ps, 2 * c + half + 1)
                    at = slice(c, c + 1) if isinstance(c, int) else bass.ds(c, 1)
                    dve.tensor_tensor(hs[:, at, half * 512:(half + 1) * 512].rearrange("p a n -> p (a n)"), gelu_s[:, half, :], ps[:, 2 * half + 1, :], ALU.mult).then_inc(hs_ready, 1)

                def pick(r):
                    dve.wait_ge(removed, r)
                    dve.memset(stand[:, :], 0.0)
                    dve.max(best8[:, :], score[:, :]).then_inc(found, 1)
                    dve.wait_ge(found, 2 * r + 1)
                    dve.memset(stand[:, :], 0.0)
                    dve.max_index(best8_at[:, :], best8[:, :], score[:, :]).then_inc(found, 1)
                    dve.wait_ge(found, 2 * r + 2)
                    dve.tensor_copy(best[:, bass.ds(r * 8, 8)], best8[:, :]).then_inc(placed, 1)
                    dve.tensor_copy(best_at[:, bass.ds(r * 8, 8)], best8_at[:, :]).then_inc(placed, 1)
                    dve.wait_ge(placed, 2 * r + 2)
                    dve.memset(stand[:, :], 0.0)
                    dve.match_replace(score[:, :], best8[:, :], score[:, :], -1.0).then_inc(removed, 1)

                gated(0, 0)
                gated(0, 1)
                dve.wait_ge(turn_ps, 1)
                dve.tensor_copy(score[:, :], ps[0:E, 4:6, :].rearrange("p a n -> p (a n)")).then_inc(score_ready, 1)
                dve.wait_ge(score_ready, 1)
                pick(0)
                pick(1)
                with dve.Fori(1, KI) as c:
                    pick(c * 2)
                    gated(c, 0)
                    pick(c * 2 + 1)
                    gated(c, 1)
                def step(gg):
                    for h_ in range(2):
                        g = gg * 2 + h_
                        dve.wait_ge(hs_hi, g + 1)
                        dve.tensor_tensor(hsl[:, 0], hs[:, :, bass.ds(g * P, P)], hsh[:, 0].bitcast(F32), ALU.subtract).then_inc(hs_lo, 1)
                        dve.wait_ge(y_out[h_], gg * 16)
                        dve.wait_ge(down_ps, g + 1)
                        dve.tensor_tensor(y[:, h_, :], x[:, bass.ds(g, 1), :].rearrange("p a n -> p (a n)"), ps[:, 6, :], ALU.add).then_inc(y_ready, 1)
                steps(dve, G // 2, step)
                dve.wait_ge(picked_ps, 1)
                dve.tensor_copy(weight[:, :], ps[:, 7, 0:E]).then_inc(token_ready, 1)
                dve.tensor_copy(token[:, :], ps[:, 7, E:2 * E]).then_inc(token_ready, 1)

                def gate_times_up(e, n):
                    dve.wait_ge(e_gelu, e * NI + n + 1)
                    dve.wait_ge(u_ps, e * NI + n + 1)
                    if not (isinstance(e, int) and e == 0 and n < 2):
                        dve.wait_ge(ht_ps, e * NI + n - 1)
                    dve.tensor_tensor(h[:, n % 2, :], gelu_e[:, n % 2, :], ps[:, n % 2 * 2 + 1, :], ALU.mult).then_inc(h_ready, 1)

                def turned_hidden(e, n):
                    dve.wait_ge(ht_ps, e * NI + n + 1)
                    if not (isinstance(e, int) and e == 0 and n < 2):
                        dve.wait_ge(d_used, e * NI + n - 1)
                    dve.tensor_copy(ht[:, n % 2], ps[:, 4, :].rearrange("p (k n) -> p k n", k=4)).then_inc(ht_ready, 1)

                def expert(e, last):
                    for n in range(1, NI):
                        gate_times_up(e, n)
                        turned_hidden(e, n - 1)
                    if not last:
                        gate_times_up(e + 1, 0)
                    turned_hidden(e, NI - 1)
                    dve.wait_ge(d_used, (e + 1) * NI)
                    dve.wait_ge(scattered, e * 16)
                    at = slice(e, e + 1) if isinstance(e, int) else bass.ds(e, 1)
                    dve.tensor_scalar(eo[:, :], ps[:, 5, :], weight[:, at], None, ALU.mult).then_inc(eo_ready, 1)

                dve.wait_ge(token_ready, 2)
                gate_times_up(0, 0)
                expert(0, False)
                with dve.Fori(1, E - 1) as e:
                    expert(e, False)
                expert(E - 1, True)

            @block.gpsimd
            def _(pool):
                def split_shared(c):
                    at = slice(c, c + 1) if isinstance(c, int) else bass.ds(c, 1)
                    pool.wait_ge(sgu_hi, c + 1)
                    pool.tensor_tensor(sgul[:, :, :, :], s_raw[:, :, :, :], sguh[:, :, :, :].bitcast(F32), ALU.subtract).then_inc(sgu_lo, 1)
                    pool.wait_ge(sd_hi, c + 1)
                    pool.tensor_tensor(sdl[:, at, :].rearrange("p a n -> p (a n)"), sd_raw[:, :], sdh[:, at, :].rearrange("p a n -> p (a n)").bitcast(F32), ALU.subtract).then_inc(sd_lo, 1)

                pool.wait_ge(gate_hi, 1)
                pool.tensor_tensor(gatel[:, :, :], gate_raw[:, :, :], gateh[:, :, :].bitcast(F32), ALU.subtract).then_inc(gate_lo, 1)
                split_shared(0)
                with pool.Fori(1, KI) as c:
                    split_shared(c)

                def gather(e):
                    at = slice(e, e + 1) if isinstance(e, int) else bass.ds(e, 1)
                    pool.wait_ge(gathered, e * 16)
                    pool.tensor_copy(gather_at[:, :], token[:, at]).then_inc(gather_idx, 1)
                    pool.wait_ge(gather_idx, e + 1)
                    pool.wait_ge(xgt_ps, e)
                    pool.tensor_tensor(pool_stand[:, :], ident[:, 0:1], ident[:, 0:1], ALU.mult)
                    pool.indirect_dma_start(xg[:, :], None, xn_dram[:, :], bass.IndirectOffsetOnAxis(gather_at[:, 0:1], 0)).then_inc(gathered, 16)

                def scatter(e):
                    at = slice(e, e + 1) if isinstance(e, int) else bass.ds(e, 1)
                    pool.wait_ge(scattered, e * 16)
                    pool.tensor_copy(scatter_at[:, :], token[:, at]).then_inc(scatter_idx, 1)
                    pool.wait_ge(scatter_idx, e + 1)
                    pool.wait_ge(eo_ready, e + 1)
                    pool.tensor_tensor(pool_stand[:, :], ident[:, 0:1], ident[:, 0:1], ALU.mult)
                    pool.indirect_dma_start(out[:, :], bass.IndirectOffsetOnAxis(scatter_at[:, 0:1], 0), eo[:, :], None, compute_op=ALU.add).then_inc(scattered, 16)

                pool.wait_ge(token_ready, 2)
                for n in range(2):
                    pool.wait_ge(xn_out[n], G // 2 * 16)
                pool.wait_ge(hs_lo, G)
                gather(0)
                for n in range(2):
                    pool.wait_ge(y_out[n], G // 2 * 16)
                def step(e):
                    gather(e + 1)
                    scatter(e)
                steps(pool, E - 1, step)
                scatter(E - 1)


def perceiver_block(nc, x_dram, ctxT, ctx, mask, wq_x, wkT_x, wv_x, wo_x, bo_x, wq, wk, wv, wo, rel_bias, onehot,
                    gate, sg, su, sd, wg, wu, wd, ident_dram, rows_dram, out):
    ps = nc.alloc_psum_tensor("ps", [P, 8, 512], F32)
    xn_dram = nc.dram_tensor("layernormed", [T, D], F32, kind="Internal").ap()
    sb = Map(nc, (nc.sbuf_base + 63) // 64 * 64)
    x, ident = sb("x", [P, G, D], F32), sb("ident", [P, P], F32)
    cross_attention(nc, ps, x_dram.rearrange("b s d -> (b s) d"), ctxT, ctx, mask, wq_x, wkT_x, wv_x, wo_x, bo_x,
                    ident_dram, rows_dram, x, ident, sb.offset)
    xth, xtl = sb("all_xth", [P, KD, T], F32R), sb("all_xtl", [P, KD, T], F32R)
    self_attention(nc, ps, wq, wk, wv, wo, rel_bias, onehot, x, ident, xth, xtl, sb.offset)
    mixture(nc, ps, gate, sg, su, sd, wg, wu, wd, xn_dram, out.rearrange("b s d -> (b s) d"), x, ident, xth, xtl, sb.offset)


def bucket_onehot():
    distance = np.arange(S)[None, :] - np.arange(S)[:, None]
    half, exact, furthest = NBUCKET // 2, NBUCKET // 4, 128
    near = np.abs(distance)
    scale = np.float32(math.log(furthest / exact))
    far = exact + (np.log(np.maximum(near, 1).astype(np.float32) / np.float32(exact)) / scale * np.float32(half - exact)).astype(np.int32)
    bucket = (distance > 0) * half + np.where(near < exact, near, np.minimum(far, half - 1))
    onehot = np.zeros((NBUCKET, S, BPG, S), np.float32)
    for i in range(S):
        for j in range(S):
            onehot[bucket[i, j], j, :, i] = 1
    return onehot.reshape(NBUCKET, S * P)


def kernel(**inputs):
    import concourse.bacc as bacc
    from concourse.bass_utils import run_bass_kernel_spmd

    a = {k: np.asarray(v) for k, v in inputs.items()}
    w = lambda name: a["L0_" + name]
    columns = lambda t: t.reshape(KI, P, KD, P).transpose(0, 3, 2, 1)
    expert_columns = lambda t: t.reshape(E, NI, 512, KD, P).transpose(0, 1, 4, 3, 2)
    arrays = {
        "x": a["x"],
        "ctxT": a["ctx_768"].transpose(0, 2, 1),
        "ctx": a["ctx_768"],
        "mask": a["mask_BxS2_bk0"],
        "xattn_wq": w("xattn_W_q"), "xattn_wkT": w("xattn_W_k").T, "xattn_wv": w("xattn_W_v"), "xattn_wo": w("xattn_W_o"), "xattn_bo": w("xattn_b_o"),
        "attn_wq": w("attn_wq"), "attn_wk": w("attn_wk"), "attn_wv": w("attn_wv"), "attn_wo": w("attn_wo"), "rel_bias": w("attn_rel_bias"),
        "onehot": bucket_onehot(),
        "gate": w("ffn_gate_w").T,
        "sg": columns(w("ffn_Sg")), "su": columns(w("ffn_Su")), "sd": w("ffn_Sd").T,
        "wg": expert_columns(w("ffn_Wg")), "wu": expert_columns(w("ffn_Wu")),
        "wd": w("ffn_Wd").reshape(E, D, NI, 4, P).transpose(0, 2, 4, 3, 1),
        "ident": np.eye(P, dtype=np.float32),
        "rows": np.array([[0, 0], [-1, 0], [0, -1], [-1, -1]], np.float32),
    }
    arrays = {"in_" + k: np.ascontiguousarray(v) for k, v in arrays.items()}
    nc = bacc.Bacc("TRN2", target_bir_lowering=False, num_devices=1)
    args = [nc.dram_tensor(k, v.shape, mybir.dt.from_np(v.dtype), kind="ExternalInput").ap() for k, v in arrays.items()]
    out = nc.dram_tensor("out", [B, S, D], F32, kind="ExternalOutput").ap()
    perceiver_block(nc, *args, out)
    result = run_bass_kernel_spmd(nc, [arrays], core_ids=[0])
    return result.results[0]["out"]
```

```python
import math
from contextlib import contextmanager

import numpy as np

import concourse.bass as bass
from concourse import mybir

ALU = mybir.AluOpType
ACT = mybir.ActivationFunctionType
F32 = mybir.dt.float32
F32R = mybir.dt.float32r
U32 = mybir.dt.uint32
U8 = mybir.dt.uint8
AX_X = mybir.AxisListType.X

P = 128
B, S, D = 32, 32, 512
T = B * S
G = T // P
BPG = P // S
KD = D // P
J, CD = 257, 384
KC = CD // P
JE = J + 1
JB = J // P
XH, DH = 8, 64
XP = XH * DH // P
SH = 16
NP = SH * DH // P
NBUCKET = 32
E, C, I = 16, 128, 2048
NI = I // 512
IS = 1024
KI = IS // P
EPS = 1e-5
FLT_MAX = 3.4028234663852886e38


def products(pe, out, stationary, moving, start, stop):
    (wh, wl), (xh, xl) = stationary, moving
    pe.matmul(out, wl, xh, start=start, stop=False)
    pe.matmul(out, wh, xl, start=False, stop=False)
    return pe.matmul(out, wh, xh, start=False, stop=stop)


class Map:

    def __init__(self, nc, offset):
        self.nc, self.offset = nc, offset

    def __call__(self, name, shape, dtype, size=4):
        t = self.nc.alloc_sbuf_tensor_at(name, shape, dtype, offset=self.offset)
        self.offset += (int(np.prod(shape[1:])) * size + 31) // 32 * 32
        return t


@contextmanager
def semaphores(nc, prefix):
    taken = []

    def semaphore(name):
        taken.append(nc.alloc_semaphore(name=prefix + name))
        return taken[-1]

    yield semaphore
    nc.clear_and_free_semaphores(taken)
    nc.all_engine_barrier()


def steps(engine, count, step):
    step(0)
    with engine.Fori(1, count) as i:
        step(i)
SBUF_END = 229344


def cross_attention(nc, ps, x_dram, ctxT, ctx, mask, wq, wkT, wv, wo, bo, ident_dram, rows_dram, x, ident, stats, free):
    sb = Map(nc, free)
    wqh, wql = sb("wqh", [P, KD, D], F32R), sb("wql", [P, KD, D], F32R)
    wkh, wkl = sb("wkh", [P, XP, CD], F32R), sb("wkl", [P, XP, CD], F32R)
    wvh, wvl = sb("wvh", [P, KC, D], F32R), sb("wvl", [P, KC, D], F32R)
    woh, wol = sb("woh", [P, XP, D], F32R), sb("wol", [P, XP, D], F32R)
    raw = Map(nc, sb.offset)
    wq_raw, wk_raw = raw("wq_raw", [P, KD, D], F32), raw("wk_raw", [P, XP, CD], F32)
    wv_raw, wo_raw = raw("wv_raw", [P, KC, D], F32), raw("wo_raw", [P, XP, D], F32)
    qkh, qkl = sb("qkh", [P, KC, 2, BPG, XP, S], F32R), sb("qkl", [P, KC, 2, BPG, XP, S], F32R)
    oh, ol = sb("oh", [P, KC, 2 * XP, P], F32R), sb("ol", [P, KC, 2 * XP, P], F32R)
    xn = sb("xn", [P, D], F32)
    xth, xtl = sb("xth", [P, KD, P], F32R), sb("xtl", [P, KD, P], F32R)
    qh, ql = sb("qh", [P, XP, P], F32R), sb("ql", [P, XP, P], F32R)
    aoh, aol = sb("aoh", [P, XP, P], F32R), sb("aol", [P, XP, P], F32R)
    ctxT_raw, ctx_raw = sb("ctxT_raw", [P, 2, KC, J], F32), sb("ctx_raw", [P, 2, JB, CD], F32)
    last_raw, last_hi = sb("last_raw", [4, 2, CD], F32), sb("last_hi", [4, CD], F32R)
    cTh, cTl = sb("cTh", [P, 2, KC, JE], F32R), sb("cTl", [P, 2, KC, JE], F32R)
    ch, cl = sb("ch", [P, 2, JB, CD], F32R), sb("cl", [P, 2, JB, CD], F32R)
    last4 = sb("last4", [P, 2, CD], F32R)
    mask_all = sb("mask_all", [P, B * J], U8, 1)
    mask_bias = sb("mask_bias", [P, J], F32)
    prob = sb("prob", [P, 2, 2, J], F32)
    pth, ptl = sb("pth", [P, JB, 2 * P], F32R), sb("ptl", [P, JB, 2 * P], F32R)
    p4_hi, p4 = sb("p4_hi", [4, 2 * P], F32R), sb("p4", [P, 2 * P], F32R)
    xb = sb("xb", [P, D], F32)
    bo_sb = sb("bo_sb", [P, D], F32)
    rows, stand = sb("rows", [4, 2], F32), sb("stand", [P, 1], F32)
    mv, rstd = sb("mv", [P, G, 2], F32), sb("rstd", [P, G], F32)
    maxes, sums = sb("maxes", [P, 2, 2], F32), sb("sums", [P, 2, 2], F32)
    neg_max, inv_sum = sb("neg_max", [P, 2, 2], F32), sb("inv_sum", [P, 2, 2], F32)
    assert sb.offset <= SBUF_END, sb.offset

    QK_BANKS = (2, 3, 0, 1, 2, 3)
    pt_ps = ps[:, 4, :]
    o_ps = ps[:, 5:7, :].rearrange("p a n -> p (a n)")[:, 0:KC * 2 * P]
    p4_ps = ps[0:4, 7, 0:2 * P]

    with semaphores(nc, "a_") as sem:
        x_in, const_in, mask_in = sem("x_in"), sem("const_in"), sem("mask_in")
        w_in = [sem(f"w_in{n}") for n in range(4)]
        w_hi, w_lo, zeroed = sem("w_hi"), sem("w_lo"), sem("zeroed")
        bn_done, mv_done, var_done, std_done, rstd_done = (sem(n) for n in ("bn_done", "mv_done", "var_done", "std_done", "rstd_done"))
        ctxT_in = [sem(f"ctxT_in{n}") for n in range(2)]
        ctx_in = [sem(f"ctx_in{n}") for n in range(2)]
        ctxT_hi, ctxT_lo, ctx_hi, ctx_lo, last_ready = (sem(n) for n in ("ctxT_hi", "ctxT_lo", "ctx_hi", "ctx_lo", "last_ready"))
        bias_ready = sem("bias_ready")
        xn_ready, xt_ps, xt_hi, xt_lo = (sem(n) for n in ("xn_ready", "xt_ps", "xt_hi", "xt_lo"))
        q_ps, q_hi, q_lo = sem("q_ps"), sem("q_hi"), sem("q_lo")
        qk_ps, qk_hi, qk_lo = sem("qk_ps"), sem("qk_hi"), sem("qk_lo")
        score_ps, max_ready, neg_ready, exp_ready = (sem(n) for n in ("score_ps", "max_ready", "neg_ready", "exp_ready"))
        inv_ready, prob_ready, pt_done, pt_hi, pt_lo, p4_hi_ready, p4_ready = (
            sem(n) for n in ("inv_ready", "prob_ready", "pt_done", "pt_hi", "pt_lo", "p4_hi_ready", "p4_ready"))
        pv_done, o_hi, o_lo = sem("pv_done"), sem("o_hi"), sem("o_lo")
        wv_done, ao_hi, ao_lo, wo_done, xb_ready, x_done = (sem(n) for n in ("wv_done", "ao_hi", "ao_lo", "wo_done", "xb_ready", "x_done"))

        def load_ctxT(sp, g, b):
            n = g * BPG + b
            if not (isinstance(g, int) and n < 2):
                sp.wait_ge(ctxT_lo, sp.snap(n - 1))
            sp.dma_start(ctxT_raw[:, b % 2], ctxT[bass.ds(n, 1)].rearrange("a (k p) j -> p (a k) j", p=P)).then_inc(ctxT_in[b % 2], 16)

        def load_ctx(sp, g, b):
            n = g * BPG + b
            if not (isinstance(g, int) and n < 2):
                sp.wait_ge(ctx_lo, sp.snap(n - 1))
                sp.wait_ge(last_ready, sp.snap(n - 1))
            sp.dma_start(ctx_raw[:, b % 2], ctx[bass.ds(n, 1), 0:JB * P].rearrange("a (k p) c -> p (a k) c", p=P)).then_inc(ctx_in[b % 2], 16)
            sp.dma_start(last_raw[:, b % 2, :], ctx[bass.ds(n, 1), J - 1].to_broadcast([4, CD])).then_inc(ctx_in[b % 2], 16)

        with nc.Block() as block:
            @block.sync
            def _(sp):
                sp.dma_start(x[:, :, :], x_dram.rearrange("(g p) d -> p g d", p=P)).then_inc(x_in, 16)
                sp.dma_start(ident[:, :], ident_dram).then_inc(const_in, 16)
                sp.dma_start(rows[:, :], rows_dram).then_inc(const_in, 16)
                sp.dma_start(bo_sb[:, :], bo.rearrange("(a n) -> a n", a=1).to_broadcast([P, D])).then_inc(const_in, 16)
                sp.dma_start(wq_raw[:, :, :], wq.rearrange("(k p) n -> p k n", p=P)).then_inc(w_in[0], 16)
                sp.dma_start(wk_raw[:, :, :], wkT.rearrange("(k p) n -> p k n", p=P)).then_inc(w_in[1], 16)
                sp.dma_start(wv_raw[:, :, :], wv.rearrange("(k p) n -> p k n", p=P)).then_inc(w_in[2], 16)
                sp.dma_start(wo_raw[:, :, :], wo.rearrange("(k p) n -> p k n", p=P)).then_inc(w_in[3], 16)
                load_ctxT(sp, 0, 0)
                sp.dma_start(mask_all[:, :], mask.rearrange("b j -> (b j)").rearrange("(a n) -> a n", a=1).to_broadcast([P, B * J])).then_inc(mask_in, 16)
                load_ctx(sp, 0, 0)
                load_ctxT(sp, 0, 1)
                load_ctxT(sp, 0, 2)
                load_ctx(sp, 0, 1)

                def group(g, last):
                    if not isinstance(g, int) or g:
                        load_ctx(sp, g, 1)
                    load_ctxT(sp, g, 3)
                    if not last:
                        load_ctxT(sp, g, 4)
                    load_ctx(sp, g, 2)
                    if not last:
                        load_ctxT(sp, g, 5)
                    load_ctx(sp, g, 3)
                    if not last:
                        load_ctx(sp, g, 4)
                        load_ctxT(sp, g, 6)

                group(0, False)
                with sp.Fori(1, G - 1) as g:
                    group(g, False)
                group(G - 1, True)

            @block.tensor
            def _(pe):
                def turn_tokens(g):
                    pe.wait_ge(xn_ready, g + 1)
                    for k in range(KD):
                        mm = pe.transpose(ps[:, 2, k * P:(k + 1) * P], xn[:, k * P:(k + 1) * P], ident[:, :])
                    mm.then_inc(xt_ps, 1)

                def queries(g):
                    pe.wait_ge(xt_lo, g + 1)
                    for m in range(XP):
                        for k in range(KD):
                            at = slice(m * P, (m + 1) * P)
                            mm = products(pe, ps[:, 0, at], (wqh[:, k, at], wql[:, k, at]), (xth[:, k, :], xtl[:, k, :]), k == 0, k == KD - 1)
                    mm.then_inc(q_ps, 1)

                def absorb(g, c):
                    pe.wait_ge(q_lo, g + 1)
                    if c == KC - 1:
                        pe.wait_ge(qk_lo, g * 2 * KC + 2)
                    for m in range(XP):
                        for s in range(2):
                            half = slice(s * DH, (s + 1) * DH)
                            mm = products(pe, ps[:, QK_BANKS[2 * c + s], m * P:(m + 1) * P],
                                          [t[half, m, c * P:(c + 1) * P] for t in (wkh, wkl)],
                                          [t[half, m, :] for t in (qh, ql)], True, True)
                    mm.then_inc(qk_ps, 1)

                def scores(g, b):
                    n = g * BPG + b
                    par = b % 2
                    pe.wait_ge(ctxT_lo, n + 1)
                    if b < 2:
                        pe.wait_ge(qk_lo, (g + 1) * 2 * KC)
                    else:
                        pe.wait_ge(max_ready, n - 1)
                    for s in range(2):
                        for c in range(KC):
                            w = [t[:, c, s, b].rearrange("p m i -> p (m i)") for t in (qkh, qkl)]
                            mm = products(pe, ps[:, 2 * par + s, 0:JE], w, (cTh[:, par, c, :], cTl[:, par, c, :]), c == 0, c == KC - 1)
                    mm.then_inc(score_ps, 1)

                def turn_probs(g, b):
                    n = g * BPG + b
                    pe.wait_ge(prob_ready, n + 1)
                    pe.wait_ge(p4_ready, n)
                    if b == 0:
                        pe.wait_ge(ao_lo, 2 * g)
                    for s in range(2):
                        for jb in range(JB):
                            pe.transpose(pt_ps[:, jb * 2 * P + s * P:jb * 2 * P + (s + 1) * P], prob[:, b % 2, s, jb * P:(jb + 1) * P], ident[:, :])
                        mm = pe.transpose(p4_ps[:, s * P:(s + 1) * P], prob[:, b % 2, s, J - 1:J].to_broadcast([P, 4]), ident[:, :])
                    mm.then_inc(pt_done, 1)

                def attend(g, b):
                    n = g * BPG + b
                    par = b % 2
                    pe.wait_ge(ctx_lo, n + 1)
                    pe.wait_ge(last_ready, n + 1)
                    pe.wait_ge(p4_ready, n + 1)
                    pe.wait_ge(o_lo, n)
                    if b == 0:
                        pe.wait_ge(x_done, g)
                    for c in range(KC):
                        at = slice(c * P, (c + 1) * P)
                        out = o_ps[:, c * 2 * P:(c + 1) * 2 * P]
                        for jb in range(JB):
                            products(pe, out, (ch[:, par, jb, at], cl[:, par, jb, at]), (pth[:, jb, :], ptl[:, jb, :]), jb == 0, False)
                        mm = pe.matmul(out, last4[:, par, at], p4[:, :], start=False, stop=True)
                    mm.then_inc(pv_done, 1)

                def values(g):
                    pe.wait_ge(o_lo, (g + 1) * BPG)
                    for m in range(XP):
                        for s in range(2):
                            at = slice((2 * m + s) * DH, (2 * m + s + 1) * DH)
                            for c in range(KC):
                                mm = products(pe, ps[0:DH, 4 if s else 7, m * P:(m + 1) * P],
                                              (wvh[:, c, at], wvl[:, c, at]),
                                              (oh[:, c, s * XP + m, :], ol[:, c, s * XP + m, :]), c == 0, c == KC - 1)
                    mm.then_inc(wv_done, 1)

                def project(g):
                    pe.wait_ge(ao_lo, 2 * g + 2)
                    for m in range(XP):
                        mm = products(pe, ps[:, 5, :], (aoh[:, m, :], aol[:, m, :]), (woh[:, m, :], wol[:, m, :]), m == 0, m == XP - 1)
                    mm.then_inc(wo_done, 1)

                def group(g, last):
                    turn_probs(g, 0)
                    scores(g, 2)
                    if not last:
                        turn_tokens(g + 1)
                    attend(g, 0)
                    turn_probs(g, 1)
                    if not last:
                        pe.wait_ge(xt_lo, g + 2)
                    scores(g, 3)
                    if not last:
                        pe.wait_ge(max_ready, g * BPG + 3)
                        queries(g + 1)
                    attend(g, 1)
                    turn_probs(g, 2)
                    if not last:
                        pe.wait_ge(max_ready, g * BPG + 4)
                        absorb(g + 1, 0)
                        absorb(g + 1, 1)
                    attend(g, 2)
                    turn_probs(g, 3)
                    if not last:
                        absorb(g + 1, 2)
                    attend(g, 3)
                    if not last:
                        scores(g + 1, 0)
                    values(g)
                    if not last:
                        scores(g + 1, 1)
                    project(g)

                pe.wait_ge(const_in, 48)
                turn_tokens(0)
                pe.wait_ge(w_lo, 1)
                queries(0)
                pe.wait_ge(zeroed, 4)
                pe.wait_ge(w_lo, 4)
                for c in range(KC):
                    absorb(0, c)
                scores(0, 0)
                scores(0, 1)
                def step(g):
                    group(g, False)
                steps(pe, G - 1, step)
                group(G - 1, True)

            @block.scalar
            def _(act):
                def split_ctxT(g, b):
                    act.wait_ge(ctxT_in[b % 2], (g * (BPG // 2) + b // 2 + 1) * 16)
                    act.activation(cTh[:, b % 2, :, 0:J], ctxT_raw[:, b % 2], ACT.Copy).then_inc(ctxT_hi, 1)

                def split_ctx(g, b):
                    act.wait_ge(ctx_in[b % 2], (g * (BPG // 2) + b // 2 + 1) * 32)
                    act.activation(ch[:, b % 2, :, :], ctx_raw[:, b % 2], ACT.Copy).then_inc(ctx_hi, 1)
                    act.wait_ge(last_ready, g * BPG + b)
                    act.activation(last_hi[:, :], last_raw[:, b % 2, :], ACT.Copy).then_inc(ctx_hi, 1)

                def exponentials(g, b):
                    n = g * BPG + b
                    act.wait_ge(neg_ready, n + 1)
                    for s in range(2):
                        row = prob[:, b % 2, s, :]
                        mm = act.activation(row, row, ACT.Exp, bias=neg_max[:, b % 2, s:s + 1], accum_out=sums[:, b % 2, s:s + 1])
                    mm.then_inc(exp_ready, 1)

                def split_probs(g, b):
                    act.wait_ge(pt_done, g * BPG + b + 1)
                    act.activation(pth[:, :, :], pt_ps.rearrange("p (k n) -> p k n", k=JB), ACT.Copy).then_inc(pt_hi, 1)
                    act.activation(p4_hi[:, :], p4_ps, ACT.Copy).then_inc(p4_hi_ready, 1)

                def split_out(g, b):
                    act.wait_ge(pv_done, g * BPG + b + 1)
                    act.activation(oh[:, :, :, b * S:(b + 1) * S].rearrange("p c h n -> p (c h) n"),
                                   o_ps.rearrange("p (q n) -> p q n", n=S), ACT.Copy).then_inc(o_hi, 1)

                def split_tokens(g):
                    act.wait_ge(xt_ps, g + 1)
                    act.activation(xth[:, :, :], ps[:, 2, :].rearrange("p (k n) -> p k n", k=KD), ACT.Copy).then_inc(xt_hi, 1)

                def split_queries(g):
                    act.wait_ge(q_ps, g + 1)
                    act.activation(qh[:, :, :], ps[:, 0, :].rearrange("p (k n) -> p k n", k=XP), ACT.Copy, scale=DH ** -0.5).then_inc(q_hi, 1)

                def split_absorbed(g, c):
                    act.wait_ge(qk_ps, g * KC + c + 1)
                    for s in range(2):
                        act.activation(qkh[:, c, s].rearrange("p b m i -> p m b i"),
                                       ps[:, QK_BANKS[2 * c + s], :].rearrange("p (m b i) -> p m b i", m=XP, b=BPG), ACT.Copy).then_inc(qk_hi, 1)

                def group(g, last):
                    split_probs(g, 0)
                    split_ctx(g, 1)
                    split_ctxT(g, 3)
                    exponentials(g, 2)
                    if not last:
                        split_tokens(g + 1)
                        split_ctxT(g, 4)
                    split_out(g, 0)
                    split_probs(g, 1)
                    split_ctx(g, 2)
                    exponentials(g, 3)
                    if not last:
                        split_queries(g + 1)
                        split_ctxT(g, 5)
                    split_out(g, 1)
                    split_probs(g, 2)
                    if not last:
                        split_absorbed(g + 1, 0)
                        split_absorbed(g + 1, 1)
                    split_ctx(g, 3)
                    split_out(g, 2)
                    split_probs(g, 3)
                    if not last:
                        split_absorbed(g + 1, 2)
                        split_ctx(g, 4)
                    split_out(g, 3)
                    if not last:
                        exponentials(g, 4)
                        split_ctxT(g, 6)
                    act.wait_ge(wv_done, g + 1)
                    for s in range(2):
                        act.activation(aoh[s * DH:(s + 1) * DH, :, :], ps[0:DH, 4 if s else 7, :].rearrange("p (m n) -> p m n", m=XP), ACT.Copy).then_inc(ao_hi, 1)
                    if not last:
                        exponentials(g, 5)

                act.wait_ge(var_done, 1)
                act.activation(rstd[:, :], rstd[:, :], ACT.Sqrt).then_inc(std_done, 1)

                def split_weights(n, hi, w):
                    act.wait_ge(w_in[n], 16)
                    act.activation(hi[:, :, :], w[:, :, :], ACT.Copy).then_inc(w_hi, 1)

                split_weights(0, wqh, wq_raw)
                split_tokens(0)
                split_weights(1, wkh, wk_raw)
                split_weights(2, wvh, wv_raw)
                split_weights(3, woh, wo_raw)
                split_queries(0)
                split_ctxT(0, 0)
                split_ctxT(0, 1)
                for c in range(KC):
                    split_absorbed(0, c)
                split_ctx(0, 0)
                exponentials(0, 0)
                split_ctxT(0, 2)
                exponentials(0, 1)
                with act.Fori(0, G - 1) as g:
                    group(g, False)
                group(G - 1, True)

            @block.vector
            def _(dve):
                def last_row(g, b):
                    n = g * BPG + b
                    dve.wait_ge(ctx_hi, 2 * n + 2)
                    dve.scalar_tensor_tensor(last4[0:4, b % 2, :], last_hi[:, :].bitcast(F32), rows[:, 0:1], last_raw[:, b % 2, :], ALU.mult, ALU.add).then_inc(last_ready, 1)

                def masked_max(g, b):
                    n = g * BPG + b
                    par = b % 2
                    dve.wait_ge(max_ready, n)
                    dve.tensor_scalar(mask_bias[:, :], mask_all[:, bass.ds(n * J, J)], FLT_MAX, -FLT_MAX, ALU.mult, ALU.add).then_inc(bias_ready, 1)
                    dve.wait_ge(score_ps, n + 1)
                    dve.wait_ge(bias_ready, n + 1)
                    if not (isinstance(g, int) and n < 2):
                        dve.wait_ge(pt_done, n - 1)
                    dve.memset(stand[:, :], 0.0)
                    for s in range(2):
                        mm = dve.tensor_tensor_reduce(prob[:, par, s, :], ps[:, 2 * par + s, 0:J], mask_bias[:, :], 1.0, -FLT_MAX,
                                                      ALU.add, ALU.max, maxes[:, par, s:s + 1])
                    mm.then_inc(max_ready, 1)
                    dve.wait_ge(max_ready, n + 1)
                    dve.tensor_scalar(neg_max[:, par, :], maxes[:, par, :], -1.0, None, ALU.mult).then_inc(neg_ready, 1)

                def normalise(g, b):
                    n = g * BPG + b
                    par = b % 2
                    dve.wait_ge(exp_ready, n + 1)
                    dve.reciprocal(inv_sum[:, par, :], sums[:, par, :]).then_inc(inv_ready, 1)
                    dve.wait_ge(inv_ready, n + 1)
                    for s in range(2):
                        row = prob[:, par, s, :]
                        mm = dve.tensor_scalar(row, row, inv_sum[:, par, s:s + 1], None, ALU.mult)
                    mm.then_inc(prob_ready, 1)

                dve.memset(cTh[:, :, :, J:JE].bitcast(F32), 0.0).then_inc(zeroed, 1)
                dve.memset(cTl[:, :, :, J:JE].bitcast(F32), 0.0).then_inc(zeroed, 1)
                dve.memset(last4[:, :, :].bitcast(F32), 0.0).then_inc(zeroed, 1)
                dve.memset(p4[:, :].bitcast(F32), 0.0).then_inc(zeroed, 1)
                dve.wait_ge(x_in, 16)
                for g in range(G):
                    dve.bn_stats(stats[:, g, :], x[:, g, :]).then_inc(bn_done, 1)
                dve.wait_ge(bn_done, G)
                for g in range(G):
                    dve.bn_aggr(mv[:, g, :], stats[:, g, :]).then_inc(mv_done, 1)
                dve.wait_ge(mv_done, G)
                dve.tensor_scalar(rstd[:, :], mv[:, :, 1], EPS, None, ALU.add).then_inc(var_done, 1)
                dve.wait_ge(std_done, 1)
                dve.reciprocal(rstd[:, :], rstd[:, :]).then_inc(rstd_done, 1)
                dve.wait_ge(const_in, 48)
                dve.wait_ge(zeroed, 4)
                dve.wait_ge(rstd_done, 1)

                def center(g):
                    at = slice(g, g + 1) if isinstance(g, int) else bass.ds(g, 1)
                    dve.wait_ge(xt_ps, g)
                    xg = x[:, at, :].rearrange("p a n -> p (a n)")
                    dve.tensor_scalar(xn[:, :], xg, mv[:, at, 0], rstd[:, at], ALU.subtract, ALU.mult).then_inc(xn_ready, 1)

                def split_tokens(g):
                    dve.wait_ge(xt_hi, g + 1)
                    dve.tensor_tensor(xtl[:, :, :], ps[:, 2, :].rearrange("p (k n) -> p k n", k=KD), xth[:, :, :].bitcast(F32), ALU.subtract).then_inc(xt_lo, 1)

                def split_queries(g):
                    dve.wait_ge(q_hi, g + 1)
                    dve.scalar_tensor_tensor(ql[:, :, :], ps[:, 0, :].rearrange("p (k n) -> p k n", k=XP), DH ** -0.5, qh[:, :, :].bitcast(F32), ALU.mult, ALU.subtract).then_inc(q_lo, 1)

                def split_absorbed(g, c):
                    for s in range(2):
                        dve.wait_ge(qk_hi, g * 2 * KC + 2 * c + s + 1)
                        dve.tensor_tensor(qkl[:, c, s].rearrange("p b m i -> p m b i"), ps[:, QK_BANKS[2 * c + s], :].rearrange("p (m b i) -> p m b i", m=XP, b=BPG),
                                          qkh[:, c, s].rearrange("p b m i -> p m b i").bitcast(F32), ALU.subtract).then_inc(qk_lo, 1)

                def split_probs(g, b):
                    dve.wait_ge(pt_hi, g * BPG + b + 1)
                    dve.tensor_tensor(ptl[:, :, :], pt_ps.rearrange("p (k n) -> p k n", k=JB), pth[:, :, :].bitcast(F32), ALU.subtract).then_inc(pt_lo, 1)
                    dve.wait_ge(p4_hi_ready, g * BPG + b + 1)
                    dve.scalar_tensor_tensor(p4[0:4, :], p4_hi[:, :].bitcast(F32), rows[:, 1:2], p4_ps, ALU.mult, ALU.add).then_inc(p4_ready, 1)

                def split_out(g, b):
                    dve.wait_ge(o_hi, g * BPG + b + 1)
                    at = slice(b * S, (b + 1) * S)
                    dve.tensor_tensor(ol[:, :, :, at].rearrange("p c h n -> p (c h) n"), o_ps.rearrange("p (q n) -> p q n", n=S),
                                      oh[:, :, :, at].rearrange("p c h n -> p (c h) n").bitcast(F32), ALU.subtract).then_inc(o_lo, 1)

                def group(g, last):
                    at = slice(g, g + 1) if isinstance(g, int) else bass.ds(g, 1)
                    xg = x[:, at, :].rearrange("p a n -> p (a n)")
                    dve.wait_ge(x_done, g)
                    dve.tensor_tensor(xb[:, :], xg, bo_sb[:, :], ALU.add).then_inc(xb_ready, 1)
                    split_probs(g, 0)
                    if not last:
                        center(g + 1)
                    last_row(g, 1)
                    masked_max(g, 2)
                    normalise(g, 2)
                    if not last:
                        split_tokens(g + 1)
                    split_out(g, 0)
                    split_probs(g, 1)
                    last_row(g, 2)
                    masked_max(g, 3)
                    normalise(g, 3)
                    if not last:
                        split_queries(g + 1)
                    split_out(g, 1)
                    split_probs(g, 2)
                    if not last:
                        split_absorbed(g + 1, 0)
                        split_absorbed(g + 1, 1)
                    last_row(g, 3)
                    split_out(g, 2)
                    split_probs(g, 3)
                    if not last:
                        split_absorbed(g + 1, 2)
                        last_row(g, 4)
                    split_out(g, 3)
                    if not last:
                        masked_max(g, 4)
                        normalise(g, 4)
                    for s in range(2):
                        dve.wait_ge(ao_hi, 2 * g + s + 1)
                        rows_ = slice(s * DH, (s + 1) * DH)
                        dve.tensor_tensor(aol[rows_, :, :], ps[0:DH, 4 if s else 7, :].rearrange("p (m n) -> p m n", m=XP), aoh[rows_, :, :].bitcast(F32), ALU.subtract).then_inc(ao_lo, 1)
                    if not last:
                        masked_max(g, 5)
                        normalise(g, 5)
                    dve.wait_ge(wo_done, g + 1)
                    dve.wait_ge(xb_ready, g + 1)
                    dve.tensor_tensor(xg, ps[:, 5, :], xb[:, :], ALU.add).then_inc(x_done, 1)
                    dve.wait_ge(x_done, g + 1)
                    dve.memset(stand[:, :], 0.0)
                    dve.bn_stats(stats[:, at, :].rearrange("p a n -> p (a n)"), xg)

                center(0)

                def split_weights(n, hi, lo, w):
                    dve.wait_ge(w_hi, n + 1)
                    dve.tensor_tensor(lo[:, :, :], w[:, :, :], hi[:, :, :].bitcast(F32), ALU.subtract).then_inc(w_lo, 1)

                split_weights(0, wqh, wql, wq_raw)
                split_tokens(0)
                split_weights(1, wkh, wkl, wk_raw)
                split_weights(2, wvh, wvl, wv_raw)
                split_weights(3, woh, wol, wo_raw)
                split_queries(0)
                for c in range(KC):
                    split_absorbed(0, c)
                last_row(0, 0)
                dve.wait_ge(mask_in, 16)
                masked_max(0, 0)
                normalise(0, 0)
                masked_max(0, 1)
                normalise(0, 1)
                def step(g):
                    group(g, False)
                steps(dve, G - 1, step)
                group(G - 1, True)

            @block.gpsimd
            def _(pool):
                def split_ctxT(g, b):
                    n = g * BPG + b
                    pool.wait_ge(ctxT_hi, n + 1)
                    pool.tensor_tensor(cTl[:, b % 2, :, 0:J], ctxT_raw[:, b % 2], cTh[:, b % 2, :, 0:J].bitcast(F32), ALU.subtract).then_inc(ctxT_lo, 1)

                def split_ctx(g, b):
                    pool.wait_ge(ctx_hi, 2 * (g * BPG + b) + 1)
                    pool.tensor_tensor(cl[:, b % 2, :, :], ctx_raw[:, b % 2], ch[:, b % 2, :, :].bitcast(F32), ALU.subtract).then_inc(ctx_lo, 1)

                def group(g, last):
                    split_ctx(g, 1)
                    split_ctxT(g, 3)
                    if not last:
                        split_ctxT(g, 4)
                    split_ctx(g, 2)
                    if not last:
                        split_ctxT(g, 5)
                    split_ctx(g, 3)
                    if not last:
                        split_ctx(g, 4)
                        split_ctxT(g, 6)

                split_ctxT(0, 0)
                split_ctxT(0, 1)
                split_ctx(0, 0)
                split_ctxT(0, 2)
                with pool.Fori(0, G - 1) as g:
                    group(g, False)
                group(G - 1, True)


def self_attention(nc, ps, wq, wk, wv, wo, rel_bias, onehot_dram, x, ident, stats, xth, xtl, free):
    sb = Map(nc, free)
    xn = sb("b_xn", [P, 2, D], F32)
    wqk_raw, wv_raw, wo_raw = sb("b_wqk_raw", [P, 2, KD, P], F32), sb("b_wv_raw", [P, KD, P], F32), sb("b_wo_raw", [P, D], F32)
    wqkh, wqkl = sb("b_wqkh", [P, 2, KD, P], F32R), sb("b_wqkl", [P, 2, KD, P], F32R)
    wvh, wvl = sb("b_wvh", [P, KD, P], F32R), sb("b_wvl", [P, KD, P], F32R)
    woh, wol = sb("b_woh", [P, NP, D], F32R), sb("b_wol", [P, NP, D], F32R)
    qkh, qkl = sb("b_qkh", [P, 2, T], F32R), sb("b_qkl", [P, 2, T], F32R)
    vt = sb("b_vt", [P, T], F32)
    vh, vl = sb("b_vh", [P, G, P], F32R), sb("b_vl", [P, G, P], F32R)
    prob = sb("b_prob", [P, 2, G, S], F32)
    block_prob = sb("b_block_prob", [P, 2, G, P], F32)
    ao = sb("b_ao", [P, NP, T], F32)
    bias = sb("b_bias", [P, SH, S], F32)
    maxes, sums = sb("b_maxes", [P, 2, G], F32), sb("b_sums", [P, 2, G], F32)
    stand = sb("b_stand", [P, 1], F32)
    mv, rstd = sb("b_mv", [P, G, 2], F32), sb("b_rstd", [P, G], F32)
    rel = sb("b_rel", [NBUCKET, SH], F32)
    onehot = nc.alloc_sbuf_tensor_at("b_onehot", [NBUCKET, S * P], F32, offset=sb.offset)
    pth, ptl = sb("b_pth", [P, 2, G, P], F32R), sb("b_ptl", [P, 2, G, P], F32R)
    final = Map(nc, sb.offset - 2 * G * P * 8)
    aoh, aol = final("b_aoh", [P, 2, NP, P], F32R), final("b_aol", [P, 2, NP, P], F32R)
    assert sb.offset <= SBUF_END, sb.offset

    units = ps[:, 0:4, :].rearrange("p a n -> p (a n)").rearrange("p (s g n) -> p s g n", s=2, g=G)

    with semaphores(nc, "b_") as sem:
        rel_in, bias_ps, bias_ready, zeroed = sem("rel_in"), sem("bias_ps"), sem("bias_ready"), sem("zeroed")
        mv_done, var_done, std_done, rstd_done = (sem(n) for n in ("mv_done", "var_done", "std_done", "rstd_done"))
        xn_ready, xt_ps, xt_hi, xt_lo = (sem(n) for n in ("xn_ready", "xt_ps", "xt_hi", "xt_lo"))
        wqk_in, wv_in, wo_in = sem("wqk_in"), sem("wv_in"), sem("wo_in")
        wqk_hi, wqk_lo, wv_hi, wv_lo, wo_hi, wo_lo = (sem(n) for n in ("wqk_hi", "wqk_lo", "wv_hi", "wv_lo", "wo_hi", "wo_lo"))
        score_ps, score_read, max_done, shifted, exp_done = (sem(n) for n in ("score_ps", "score_read", "max_done", "shifted", "exp_done"))
        sum_done, inv_done, prob_ready = sem("sum_done"), sem("inv_done"), sem("prob_ready")
        vt_ps, vt_ready = sem("vt_ps"), sem("vt_ready")
        v_ps, v_hi, v_lo, q_ps, k_ps, qk_hi, qk_lo = (sem(n) for n in ("v_ps", "v_hi", "v_lo", "q_ps", "k_ps", "qk_hi", "qk_lo"))
        pt_ps, pt_hi, pt_lo, pv_ps, ao_even, ao_odd = (sem(n) for n in ("pt_ps", "pt_hi", "pt_lo", "pv_ps", "ao_even", "ao_odd"))
        fin_hi, fin_lo, proj_ps, x_done = (sem(n) for n in ("fin_hi", "fin_lo", "proj_ps", "x_done"))

        with nc.Block() as block:
            @block.sync
            def _(sp):
                def load_wqk(p):
                    sp.wait_ge(wqk_lo, p)
                    at = bass.ds(p % NP * P, P) if isinstance(p, int) else bass.ds(sp.snap(p % NP * P), P)
                    sp.dma_start(wqk_raw[:, 0], wq[:, at].rearrange("(k p) n -> p k n", p=P)).then_inc(wqk_in, 16)
                    sp.dma_start(wqk_raw[:, 1], wk[:, at].rearrange("(k p) n -> p k n", p=P)).then_inc(wqk_in, 16)

                def load_wv(p):
                    sp.wait_ge(wv_lo, p)
                    sp.dma_start(wv_raw[:, :, :], wv[:, bass.ds(p % NP * P, P) if isinstance(p, int) else bass.ds(sp.snap(p % NP * P), P)].rearrange("(k p) n -> p k n", p=P)).then_inc(wv_in, 16)

                load_wqk(0)
                sp.dma_start(rel[:, :], rel_bias).then_inc(rel_in, 16)
                sp.dma_start(onehot[:, :], onehot_dram).then_inc(rel_in, 16)
                load_wv(0)
                load_wqk(1)
                def step(p):
                    two_on, one_on, here = (sp.snap(p + n) for n in (2, 1, 0)) if not isinstance(p, int) else (2, 1, 0)
                    load_wqk(two_on)
                    load_wv(one_on)
                    sp.wait_ge(wo_lo, here)
                    sp.dma_start(wo_raw[:, :], wo[bass.ds(p * P, P) if isinstance(p, int) else bass.ds(sp.snap(p * P), P), :]).then_inc(wo_in, 16)
                steps(sp, NP, step)

            @block.tensor
            def _(pe):
                def projected(p, a, half):
                    for k in range(KD):
                        at = slice(half * 512, (half + 1) * 512)
                        mm = products(pe, ps[:, (6, 4)[a] + half, :], (wqkh[:, a, k, :], wqkl[:, a, k, :]), (xth[:, k, at], xtl[:, k, at]), k == 0, k == KD - 1)
                    mm.then_inc((q_ps, k_ps)[a], 1)

                def pair(p, last):
                    pe.wait_ge(qk_lo, 4 * p + 4)
                    pe.wait_ge(pt_lo, 4 * p)
                    for g in range(G):
                        for s in range(2):
                            half, at = slice(s * DH, (s + 1) * DH), slice(g * P, (g + 1) * P)
                            mm = products(pe, units[:, s, g, :], [t[half, 0, at] for t in (qkh, qkl)], [t[half, 1, at] for t in (qkh, qkl)], True, True)
                    mm.then_inc(score_ps, 1)
                    pe.wait_ge(wv_lo, p + 1)
                    pe.wait_ge(ao_even, p)
                    for half in range(2):
                        for k in range(KD):
                            at = slice(half * 512, (half + 1) * 512)
                            mm = products(pe, ps[:, 4 + half, :], (wvh[:, k, :], wvl[:, k, :]), (xth[:, k, at], xtl[:, k, at]), k == 0, k == KD - 1)
                        mm.then_inc(vt_ps, 1)
                    if not last:
                        pe.wait_ge(wqk_lo, p + 2)
                        pe.wait_ge(ao_odd, p)
                        projected(p + 1, 0, 0)
                        projected(p + 1, 0, 1)
                    for g in range(G):
                        if g % 4 == 0:
                            pe.wait_ge(vt_ready, 2 * p + g // 4 + 1)
                        mm = pe.transpose(ps[:, 4 + g // 4, g % 4 * P:(g % 4 + 1) * P], vt[:, g * P:(g + 1) * P], ident[:, :])
                        if g % 4 == 3:
                            mm.then_inc(v_ps, 1)
                    pe.wait_ge(prob_ready, p + 1)
                    for s in range(2):
                        for g in range(G):
                            mm = pe.transpose(units[:, s, g, :], block_prob[:, s, g, :], ident[:, :])
                            if g % 4 == 3:
                                mm.then_inc(pt_ps, 1)
                    if not last:
                        pe.wait_ge(v_lo, 2 * p + 2)
                        projected(p + 1, 1, 0)
                        projected(p + 1, 1, 1)
                    pe.wait_ge(pt_lo, 4 * p + 4)
                    if last:
                        pe.wait_ge(v_lo, 2 * p + 2)
                    for s in (1, 0):
                        if not last:
                            pe.wait_ge(qk_lo, 4 * p + (6 if s else 8))
                        elif s:
                            pe.wait_ge(ao_odd, p)
                        for g in range(G):
                            mm = products(pe, ps[0:DH, (4, 6)[s] + g // 4, g % 4 * P:(g % 4 + 1) * P],
                                          [t[:, g, s * DH:(s + 1) * DH] for t in (vh, vl)], (pth[:, s, g, :], ptl[:, s, g, :]), True, True)
                        mm.then_inc(pv_ps, 1)

                def step(gg):
                    for h in range(2):
                        g = gg * 2 + h
                        pe.wait_ge(xn_ready, g + 1)
                        if not isinstance(gg, int):
                            pe.wait_ge(xt_lo, g - 1)
                        for k in range(KD):
                            mm = pe.transpose(ps[:, h, k * P:(k + 1) * P], xn[:, h, k * P:(k + 1) * P], ident[:, :])
                        mm.then_inc(xt_ps, 1)
                steps(pe, G // 2, step)
                pe.wait_ge(rel_in, 32)
                for j in range(S):
                    mm = pe.matmul(ps[:, 7, j * SH:(j + 1) * SH], onehot[:, j * P:(j + 1) * P], rel[:, :], start=True, stop=True)
                mm.then_inc(bias_ps, 1)
                pe.wait_ge(wqk_lo, 1)
                pe.wait_ge(bias_ready, 1)
                for half in range(2):
                    pe.wait_ge(xt_lo, 4 * half + 4)
                    projected(0, 0, half)
                    projected(0, 1, half)
                def step(p):
                    pair(p, False)
                steps(pe, NP - 1, step)
                pair(NP - 1, True)
                pe.wait_ge(wo_lo, NP)
                def step(gg):
                    for h in range(2):
                        g = gg * 2 + h
                        pe.wait_ge(fin_lo, g + 1)
                        if not isinstance(gg, int):
                            pe.wait_ge(x_done, g - 1)
                        for k in range(NP):
                            mm = products(pe, ps[:, h, :], (aoh[:, h, k, :], aol[:, h, k, :]), (woh[:, k, :], wol[:, k, :]), k == 0, k == NP - 1)
                        mm.then_inc(proj_ps, 1)
                steps(pe, G // 2, step)

            @block.scalar
            def _(act):
                def split_projected(p, a, half):
                    act.wait_ge((q_ps, k_ps)[a], 2 * p + half + 1)
                    act.activation(qkh[:, a, half * 512:(half + 1) * 512], ps[:, (6, 4)[a] + half, :], ACT.Copy).then_inc(qk_hi, 1)

                def split_values(p, n):
                    act.wait_ge(v_ps, 2 * p + n + 1)
                    act.activation(vh[:, 4 * n:4 * n + 4, :], ps[:, 4 + n, :].rearrange("p (g n) -> p g n", g=4), ACT.Copy).then_inc(v_hi, 1)

                def split_wqk(p):
                    act.wait_ge(wqk_in, (p + 1) * 32)
                    act.wait_ge(k_ps, 2 * p)
                    act.activation(wqkh[:, :, :, :], wqk_raw[:, :, :, :], ACT.Copy).then_inc(wqk_hi, 1)

                def split_wv(p):
                    act.wait_ge(wv_in, (p + 1) * 16)
                    act.wait_ge(v_ps, 2 * p)
                    act.activation(wvh[:, :, :], wv_raw[:, :, :], ACT.Copy).then_inc(wv_hi, 1)

                def copy_values(p, half):
                    act.wait_ge(vt_ps, 2 * p + half + 1)
                    act.wait_ge(v_ps, 2 * p)
                    act.activation(vt[:, half * 512:(half + 1) * 512], ps[:, 4 + half, :], ACT.Copy).then_inc(vt_ready, 1)

                def pair(p, last):
                    copy_values(p, 0)
                    act.wait_ge(shifted, p + 1)
                    act.activation(prob[:, :, :, :], prob[:, :, :, :], ACT.Exp).then_inc(exp_done, 1)
                    copy_values(p, 1)
                    if not last:
                        split_projected(p + 1, 0, 0)
                        split_projected(p + 1, 0, 1)
                    split_values(p, 0)
                    split_values(p, 1)
                    for n in range(4):
                        act.wait_ge(pt_ps, 4 * p + n + 1)
                        act.activation(pth[:, n // 2, n % 2 * 4:n % 2 * 4 + 4, :], units[:, n // 2, n % 2 * 4:n % 2 * 4 + 4, :], ACT.Copy).then_inc(pt_hi, 1)
                    if not last:
                        split_projected(p + 1, 1, 0)
                        split_projected(p + 1, 1, 1)
                    at = slice(p, p + 1) if last else bass.ds(p, 1)
                    act.wait_ge(wo_in, (p + 1) * 16)
                    act.activation(woh[:, at, :].rearrange("p a n -> p (a n)"), wo_raw[:, :], ACT.Copy).then_inc(wo_hi, 1)
                    act.wait_ge(pv_ps, 2 * p + 1)
                    act.activation(ao[DH:P, at, :].rearrange("p a n -> p (a n)"), ps[0:DH, 6:8, :].rearrange("p a n -> p (a n)"), ACT.Copy).then_inc(ao_odd, 1)
                    if not last:
                        split_wv(p + 1)
                        split_wqk(p + 2)

                act.wait_ge(var_done, 1)
                act.activation(rstd[:, :], rstd[:, :], ACT.Sqrt).then_inc(std_done, 1)
                with act.Fori(0, G // 2) as gg:
                    for h in range(2):
                        g = gg * 2 + h
                        act.wait_ge(xt_ps, g + 1)
                        act.activation(xth[:, :, bass.ds(g * P, P)], ps[:, h, :].rearrange("p (k n) -> p k n", k=KD), ACT.Copy).then_inc(xt_hi, 1)
                split_wqk(0)
                act.wait_ge(bias_ps, 1)
                act.activation(bias[:, :, :].rearrange("p h j -> p j h"), ps[:, 7, :].rearrange("p (j h) -> p j h", h=SH), ACT.Copy).then_inc(bias_ready, 1)
                split_wv(0)
                for half in range(2):
                    for a in range(2):
                        split_projected(0, a, half)
                split_wqk(1)
                steps(act, NP - 1, lambda p: pair(p, False))
                pair(NP - 1, True)
                def step(gg):
                    for h in range(2):
                        g = gg * 2 + h
                        act.wait_ge(ao_even, NP)
                        act.wait_ge(ao_odd, NP)
                        if not isinstance(gg, int):
                            act.wait_ge(proj_ps, g - 1)
                        act.activation(aoh[:, h], ao[:, :, bass.ds(g * P, P)], ACT.Copy).then_inc(fin_hi, 1)
                steps(act, G // 2, step)

            @block.vector
            def _(dve):
                def split_projected(p, a, half, n):
                    dve.wait_ge(qk_hi, 4 * p + n + 1)
                    at = slice(half * 512, (half + 1) * 512)
                    dve.tensor_tensor(qkl[:, a, at], ps[:, (6, 4)[a] + half, :], qkh[:, a, at].bitcast(F32), ALU.subtract).then_inc(qk_lo, 1)

                def split_values(p, n):
                    dve.wait_ge(v_hi, 2 * p + n + 1)
                    at = slice(4 * n, 4 * n + 4)
                    dve.tensor_tensor(vl[:, at, :], ps[:, 4 + n, :].rearrange("p (g n) -> p g n", g=4), vh[:, at, :].bitcast(F32), ALU.subtract).then_inc(v_lo, 1)

                def pair(p, last):
                    heads = slice(2 * p, 2 * p + 2) if last else bass.ds(p * 2, 2)
                    dve.wait_ge(score_ps, p + 1)
                    dve.wait_ge(prob_ready, p)
                    for r in range(BPG):
                        at = slice(r * S, (r + 1) * S)
                        shared = bias[at, heads, :].rearrange("p h (a j) -> p h a j", a=1).to_broadcast([S, 2, G, S])
                        mm = dve.tensor_tensor(prob[at], units[at, :, :, at], shared, ALU.add)
                    mm.then_inc(score_read, 1)
                    dve.wait_ge(score_read, p + 1)
                    dve.tensor_reduce(maxes[:, :, :], prob[:, :, :, :], AX_X, ALU.max).then_inc(max_done, 1)
                    dve.wait_ge(max_done, p + 1)
                    dve.tensor_tensor(prob[:, :, :, :], prob[:, :, :, :], maxes[:, :, :].rearrange("p s (g a) -> p s g a", a=1).to_broadcast([P, 2, G, S]), ALU.subtract).then_inc(shifted, 1)
                    dve.wait_ge(exp_done, p + 1)
                    dve.tensor_reduce(sums[:, :, :], prob[:, :, :, :], AX_X, ALU.add).then_inc(sum_done, 1)
                    dve.wait_ge(sum_done, p + 1)
                    dve.reciprocal(sums[:, :, :], sums[:, :, :]).then_inc(inv_done, 1)
                    dve.wait_ge(inv_done, p + 1)
                    dve.wait_ge(pt_ps, 4 * p)
                    for r in range(BPG):
                        at = slice(r * S, (r + 1) * S)
                        mm = dve.tensor_tensor(block_prob[at, :, :, at], prob[at], sums[at].rearrange("p s (g a) -> p s g a", a=1).to_broadcast([S, 2, G, S]), ALU.mult)
                    mm.then_inc(prob_ready, 1)
                    if not last:
                        split_projected(p + 1, 0, 0, 0)
                        split_projected(p + 1, 0, 1, 1)
                    split_values(p, 0)
                    split_values(p, 1)
                    for n in range(4):
                        dve.wait_ge(pt_hi, 4 * p + n + 1)
                        at = slice(n % 2 * 4, n % 2 * 4 + 4)
                        dve.tensor_tensor(ptl[:, n // 2, at, :], units[:, n // 2, at, :], pth[:, n // 2, at, :].bitcast(F32), ALU.subtract).then_inc(pt_lo, 1)
                    if not last:
                        split_projected(p + 1, 1, 0, 2)
                        split_projected(p + 1, 1, 1, 3)
                    at = slice(p, p + 1) if last else bass.ds(p, 1)
                    dve.wait_ge(pv_ps, 2 * p + 2)
                    dve.tensor_copy(ao[0:DH, at, :].rearrange("p a n -> p (a n)"), ps[0:DH, 4:6, :].rearrange("p a n -> p (a n)")).then_inc(ao_even, 1)

                for g in range(G):
                    dve.bn_aggr(mv[:, g, :], stats[:, g, :]).then_inc(mv_done, 1)
                dve.wait_ge(mv_done, G)
                dve.tensor_scalar(rstd[:, :], mv[:, :, 1], EPS, None, ALU.add).then_inc(var_done, 1)
                dve.memset(block_prob[:, :, :, :], 0.0).then_inc(zeroed, 1)
                dve.wait_ge(std_done, 1)
                dve.reciprocal(rstd[:, :], rstd[:, :]).then_inc(rstd_done, 1)
                dve.wait_ge(rstd_done, 1)

                def center(gg, h):
                    g = gg * 2 + h
                    at = slice(g, g + 1) if isinstance(g, int) else bass.ds(g, 1)
                    dve.tensor_scalar(xn[:, h, :], x[:, at, :].rearrange("p a n -> p (a n)"), mv[:, at, 0], rstd[:, at], ALU.subtract, ALU.mult).then_inc(xn_ready, 1)

                def turned(gg, h):
                    g = gg * 2 + h
                    dve.wait_ge(xt_hi, g + 1)
                    at = slice(g * P, g * P + P) if isinstance(g, int) else bass.ds(g * P, P)
                    dve.tensor_tensor(xtl[:, :, at], ps[:, h, :].rearrange("p (k n) -> p k n", k=KD), xth[:, :, at].bitcast(F32), ALU.subtract).then_inc(xt_lo, 1)

                center(0, 0)
                center(0, 1)
                with dve.Fori(0, G // 2 - 1) as gg:
                    for h in range(2):
                        turned(gg, h)
                        center(gg + 1, h)
                turned(G // 2 - 1, 0)
                turned(G // 2 - 1, 1)
                for half in range(2):
                    for a in range(2):
                        split_projected(0, a, half, 2 * half + a)
                dve.wait_ge(bias_ready, 1)
                dve.wait_ge(zeroed, 1)
                def step(p):
                    pair(p, False)
                steps(dve, NP - 1, step)
                pair(NP - 1, True)
                with dve.Fori(0, G // 2) as gg:
                    for h in range(2):
                        g = gg * 2 + h
                        dve.wait_ge(fin_hi, g + 1)
                        dve.tensor_tensor(aol[:, h], ao[:, :, bass.ds(g * P, P)], aoh[:, h].bitcast(F32), ALU.subtract).then_inc(fin_lo, 1)
                        dve.wait_ge(proj_ps, g + 1)
                        xg = x[:, bass.ds(g, 1), :].rearrange("p a n -> p (a n)")
                        dve.tensor_tensor(xg, xg, ps[:, h, :], ALU.add).then_inc(x_done, 1)
                        dve.wait_ge(x_done, g + 1)
                        dve.memset(stand[:, :], 0.0)
                        dve.bn_stats(stats[:, bass.ds(g, 1), :].rearrange("p a n -> p (a n)"), xg)

            @block.gpsimd
            def _(pool):
                def split_wqk(p):
                    pool.wait_ge(wqk_hi, p + 1)
                    pool.tensor_tensor(wqkl[:, :, :, :], wqk_raw[:, :, :, :], wqkh[:, :, :, :].bitcast(F32), ALU.subtract).then_inc(wqk_lo, 1)

                def split_wv(p):
                    pool.wait_ge(wv_hi, p + 1)
                    pool.tensor_tensor(wvl[:, :, :], wv_raw[:, :, :], wvh[:, :, :].bitcast(F32), ALU.subtract).then_inc(wv_lo, 1)

                split_wqk(0)
                split_wv(0)
                split_wqk(1)
                def pair(p, last):
                    at = slice(p, p + 1) if last else bass.ds(p, 1)
                    pool.wait_ge(wo_hi, p + 1)
                    pool.tensor_tensor(wol[:, at, :].rearrange("p a n -> p (a n)"), wo_raw[:, :], woh[:, at, :].rearrange("p a n -> p (a n)").bitcast(F32), ALU.subtract).then_inc(wo_lo, 1)
                    if not last:
                        split_wv(p + 1)
                        split_wqk(p + 2)
                with pool.Fori(0, NP - 1) as p:
                    pair(p, False)
                pair(NP - 1, True)


def mixture(nc, ps, gate, sg, su, sd, wg, wu, wd, xn_dram, out, x, ident, stats, xth, xtl, x_at, free):
    sb = Map(nc, free)
    slots = sb("c_slots", [P, NI, 3, 4, 512], F32)
    EARLY = 2
    early = Map(nc, free + EARLY * 3 * 4 * 512 * 4)
    sdh, sdl = early("c_sdh", [P, KI, D], F32R), early("c_sdl", [P, KI, D], F32R)
    hsh, hsl = early("c_hsh", [P, KI, P], F32R), early("c_hsl", [P, KI, P], F32R)
    s_raw = early("c_s_raw", [P, 2, KD, P], F32)
    sd_raw = early("c_sd_raw", [P, D], F32)
    assert early.offset <= sb.offset
    hs = sb("c_hs", [P, KI, T], F32)
    sguh, sgul = sb("c_sguh", [P, 2, 2, KD, P], F32R), sb("c_sgul", [P, 2, 2, KD, P], F32R)
    hs2 = Map(nc, sb.offset - 2 * 2 * 2 * KD * P * 4)
    hsh, hsl = (hsh, hs2("c_hsh2", [P, KI, P], F32R)), (hsl, hs2("c_hsl2", [P, KI, P], F32R))
    y, xg, eo = hs2("c_y", [P, 2, D], F32), hs2("c_xg", [C, D], F32), hs2("c_eo", [C, D], F32)
    assert hs2.offset <= sb.offset
    xn = sb("c_xn", [P, 2, D], F32)
    gelu_s = sb("c_gelu_s", [P, 2, D], F32)
    mv, rstd = sb("c_mv", [P, G, 2], F32), sb("c_rstd", [P, G], F32)
    gate_raw, gateh, gatel = sb("c_gate_raw", [P, KD, E], F32), sb("c_gateh", [P, KD, E], F32R), sb("c_gatel", [P, KD, E], F32R)
    route, peak, total = sb("c_route", [P, G, E], F32), sb("c_peak", [P, G], F32), sb("c_total", [P, G], F32)
    score = sb("c_score", [E, T], F32)
    best8, best8_at = sb("c_best8", [E, 8], F32), sb("c_best8_at", [E, 8], U32)
    best, best_at = sb("c_best", [E, C], F32), sb("c_best_at", [E, C], F32)
    weight, token = sb("c_weight", [C, E], F32), sb("c_token", [C, E], U32)
    weh = nc.alloc_sbuf_tensor_at("c_weh", [P, 2, 2, 4, 512], F32R, offset=free - 2 * KD * T * 4)
    wel = nc.alloc_sbuf_tensor_at("c_wel", [P, 2, 2, 4, 512], F32R, offset=free + NI * 3 * 4 * 512 * 4)
    ex = Map(nc, x_at)
    gelu_e, h, ht = ex("c_gelu_e", [C, 2, D], F32), ex("c_h", [C, 2, D], F32), ex("c_ht", [P, 2, 4, C], F32)
    xgth, xgtl = ex("c_xgth", [P, KD, C], F32R), ex("c_xgtl", [P, KD, C], F32R)
    assert ex.offset <= x_at + G * D * 4
    gather_at, scatter_at = sb("c_gather_at", [C, 1], U32), sb("c_scatter_at", [C, 1], U32)
    stand, pool_stand = sb("c_stand", [P, 1], F32), sb("c_pool_stand", [P, 1], F32)
    assert sb.offset <= SBUF_END, sb.offset

    with semaphores(nc, "c_") as sem:
        gate_in, s_in, sd_in = sem("gate_in"), sem("s_in"), sem("sd_in")
        slot_in = [[sem(f"slot_in{n}_{a}") for a in range(3)] for n in range(NI)]
        mv_done, var_done, std_done, rstd_done = (sem(n) for n in ("mv_done", "var_done", "std_done", "rstd_done"))
        xn_ready, xt_ps, xt_hi, xt_lo = (sem(n) for n in ("xn_ready", "xt_ps", "xt_hi", "xt_lo"))
        xn_out = [sem(f"xn_out{n}") for n in range(2)]
        logit_copied, logit_turned = sem("logit_copied"), sem("logit_turned")
        gate_hi, gate_lo, logit_ps, shifted, exp_done, sum_done, inv_done, route_ready = (
            sem(n) for n in ("gate_hi", "gate_lo", "logit_ps", "shifted", "exp_done", "sum_done", "inv_done", "route_ready"))
        peak_done, turn_ps, score_ready = sem("peak_done"), sem("turn_ps"), sem("score_ready")
        found, placed, removed, picked_ps, token_ready = (sem(n) for n in ("found", "placed", "removed", "picked_ps", "token_ready"))
        sgu_hi, sgu_lo, sd_hi, sd_lo = (sem(n) for n in ("sgu_hi", "sgu_lo", "sd_hi", "sd_lo"))
        sg_ps, su_ps, s_gelu, hs_ready = (sem(n) for n in ("sg_ps", "su_ps", "s_gelu", "hs_ready"))
        hs_hi, hs_lo, down_ps, y_ready = (sem(n) for n in ("hs_hi", "hs_lo", "down_ps", "y_ready"))
        y_out = [sem(f"y_out{n}") for n in range(2)]
        gather_idx, scatter_idx, gathered, scattered = (sem(n) for n in ("gather_idx", "scatter_idx", "gathered", "scattered"))
        we_hi, we_lo, xgt_hi = sem("we_hi"), sem("we_lo"), sem("xgt_hi")
        xgt_ps, xgt_ready, g_ps, u_ps, e_gelu, h_ready, ht_ps, ht_ready, eo_ps, eo_ready = (
            sem(n) for n in ("xgt_ps", "xgt_ready", "g_ps", "u_ps", "e_gelu", "h_ready", "ht_ps", "ht_ready", "eo_ps", "eo_ready"))
        d_used = sem("d_used")

        with nc.Block() as block:
            @block.sync
            def _(sp):
                def load_shared(c):
                    sp.wait_ge(sgu_lo, c)
                    sp.dma_start(s_raw[:, 0], sg[bass.ds(c, 1)].rearrange("a p k n -> p (a k) n")).then_inc(s_in, 16)
                    sp.dma_start(s_raw[:, 1], su[bass.ds(c, 1)].rearrange("a p k n -> p (a k) n")).then_inc(s_in, 16)
                    sp.wait_ge(sd_lo, c)
                    sp.dma_start(sd_raw[:, :], sd[bass.ds(c * P, P), :]).then_inc(sd_in, 16)

                def load_slot(e, n, a):
                    w = (wg, wu, wd)[a]
                    if not isinstance(e, int):
                        e = sp.snap(e + 0)
                    sp.dma_start(slots[:, n, a], w[bass.ds(e, 1), n].rearrange("a p k n -> p (a k) n")).then_inc(slot_in[n][a], 16)

                sp.dma_start(gate_raw[:, :, :], gate.rearrange("(k p) n -> p k n", p=P)).then_inc(gate_in, 16)
                load_shared(0)
                with sp.Fori(0, G // 2) as gg:
                    counts = [sp.snap(gg * 2 + h + 1) for h in range(2)]
                    for h in range(2):
                        sp.wait_ge(xn_ready, counts[h])
                        sp.dma_start(xn_dram[bass.ds((gg * 2 + h) * P, P), :], xn[:, h, :]).then_inc(xn_out[h], 16)
                load_shared(1)
                for n in range(EARLY):
                    for a in range(3):
                        load_slot(0, n, a)
                with sp.Fori(2, KI) as c:
                    load_shared(c)
                with sp.Fori(0, G // 2) as gg:
                    counts = [sp.snap(gg * 2 + h + 1) for h in range(2)]
                    for h in range(2):
                        sp.wait_ge(y_ready, counts[h])
                        sp.dma_start(out[bass.ds((gg * 2 + h) * P, P), :], y[:, h, :]).then_inc(y_out[h], 16)
                for n in range(EARLY, NI):
                    for a in range(2):
                        load_slot(0, n, a)

                def reload(e, n):
                    for a in range(2):
                        sp.wait_ge(we_lo, after_split(e, n, a))
                        load_slot(e, n, a)

                def after_split(e, n, a):
                    v = 2 * ((e - 1) * NI + n) + a + 1
                    return v if isinstance(v, int) else sp.snap(v)

                def reload_down(e, n):
                    if not isinstance(e, int) or e:
                        v = (e - 1) * NI + n + 1
                        sp.wait_ge(d_used, v if isinstance(v, int) else sp.snap(v))
                    load_slot(e, n, 2)

                def expert_slots(e):
                    reload(e, 0)
                    reload_down(e - 1, 2)
                    reload(e, 1)
                    reload_down(e - 1, 3)
                    reload(e, 2)
                    reload_down(e, 0)
                    reload(e, 3)
                    reload_down(e, 1)

                expert_slots(1)
                with sp.Fori(2, E) as e:
                    expert_slots(e)
                reload_down(E - 1, 2)
                reload_down(E - 1, 3)
                sp.wait_ge(scattered, 16 * E)

            @block.tensor
            def _(pe):
                def hidden(c, par):
                    pe.wait_ge(sgu_lo, c + 1)
                    for half in range(2):
                        at = slice(half * 512, (half + 1) * 512)
                        for a, s in ((0, sg_ps), (1, su_ps)):
                            for k in range(KD):
                                mm = products(pe, ps[:, 2 * half + a, :], (sguh[:, par, a, k, :], sgul[:, par, a, k, :]), (xth[:, k, at], xtl[:, k, at]), k == 0, k == KD - 1)
                            mm.then_inc(s, 1)

                def step(gg):
                    for h_ in range(2):
                        g = gg * 2 + h_
                        pe.wait_ge(xn_ready, g + 1)
                        if not isinstance(gg, int):
                            pe.wait_ge(xt_lo, g - 1)
                        for k in range(KD):
                            mm = pe.transpose(ps[:, h_, k * P:(k + 1) * P], xn[:, h_, k * P:(k + 1) * P], ident[:, :])
                        mm.then_inc(xt_ps, 1)
                steps(pe, G // 2, step)
                pe.wait_ge(gate_lo, 1)
                pe.wait_ge(xt_lo, G)
                for half in range(2):
                    at = slice(half * 512, (half + 1) * 512)
                    for k in range(KD):
                        mm = products(pe, ps[0:E, 4 + half, :], (gateh[:, k, :], gatel[:, k, :]), (xth[:, k, at], xtl[:, k, at]), k == 0, k == KD - 1)
                mm.then_inc(logit_ps, 1)
                pe.wait_ge(logit_copied, 1)
                for g in range(G):
                    mm = pe.transpose(ps[:, 7, g * E:(g + 1) * E], score[:, g * P:(g + 1) * P], ident[0:E, 0:E])
                mm.then_inc(logit_turned, 1)
                hidden(0, 0)
                pe.wait_ge(route_ready, 1)
                for g in range(G):
                    mm = pe.transpose(ps[0:E, 4 + g // 4, g % 4 * P:(g % 4 + 1) * P], route[:, g, :], ident[:, :])
                mm.then_inc(turn_ps, 1)
                pe.wait_ge(hs_ready, 2)
                hidden(1, 1)
                with pe.Fori(1, KI // 2) as cc:
                    for par in range(2):
                        c = cc * 2 + par
                        pe.wait_ge(hs_ready, c * 2)
                        hidden(c, par)
                pe.wait_ge(removed, C // 8)
                pe.transpose(ps[:, 5, 0:E], best[:, :], ident[0:E, 0:E])
                pe.transpose(ps[:, 5, E:2 * E], best_at[:, :], ident[0:E, 0:E]).then_inc(picked_ps, 1)
                pe.wait_ge(sd_lo, KI)

                def step(gg):
                    for h_ in range(2):
                        g = gg * 2 + h_
                        pe.wait_ge(hs_lo, g + 1)
                        if not isinstance(gg, int):
                            pe.wait_ge(y_ready, g - 1)
                        for k in range(KI):
                            mm = products(pe, ps[:, 6 + h_, :], (hsh[h_][:, k, :], hsl[h_][:, k, :]), (sdh[:, k, :], sdl[:, k, :]), k == 0, k == KI - 1)
                        mm.then_inc(down_ps, 1)

                steps(pe, G // 2, step)
                pe.wait_ge(y_ready, G)

                def turn_rows(e):
                    pe.wait_ge(gathered, (e + 1) * 16)
                    for k in range(KD):
                        mm = pe.transpose(ps[:, 6, k * P:(k + 1) * P], xg[:, k * P:(k + 1) * P], ident[:, :])
                    mm.then_inc(xgt_ps, 1)

                def times_rows(e, n, a):
                    pe.wait_ge(we_lo, 2 * (e * NI + n) + a + 1)
                    for k in range(KD):
                        mm = products(pe, ps[:, n % 2 * 2 + a, :], (xgth[:, k, :], xgtl[:, k, :]), (weh[:, a, n % 2, k, :], wel[:, a, n % 2, k, :]), k == 0, k == KD - 1)
                    mm.then_inc((g_ps, u_ps)[a], 1)

                def turn(e, n):
                    par = n % 2
                    pe.wait_ge(h_ready, e * NI + n + 1)
                    pe.wait_ge(ht_ready, e * NI + n)
                    for k in range(4):
                        mm = pe.transpose(ps[:, 4, k * P:(k + 1) * P], h[:, par, k * P:(k + 1) * P], ident[:, :])
                    mm.then_inc(ht_ps, 1)

                def down(e, n):
                    pe.wait_ge(ht_ready, e * NI + n + 1)
                    pe.wait_ge(slot_in[n][2], (e + 1) * 16)
                    if n == 0:
                        pe.wait_ge(eo_ready, e)
                    for k in range(4):
                        mm = pe.matmul(ps[:, 5, :], ht[:, n % 2, k, :], slots[:, n, 2, k, :], start=(n == 0 and k == 0), stop=(n == NI - 1 and k == 3))
                    mm.then_inc(d_used, 1)

                def expert(e, first, last):
                    pe.wait_ge(xgt_ready, e + 1)
                    for n in range(NI):
                        before = (e, n - 1) if n else (e - 1, NI - 1)
                        times_rows(e, n, 0)
                        if n or not first:
                            turn(*before)
                        times_rows(e, n, 1)
                        if n == NI - 1 and not last:
                            turn_rows(e + 1)
                        if n or not first:
                            down(*before)

                turn_rows(0)
                expert(0, True, False)
                with pe.Fori(1, E - 1) as e:
                    expert(e, False, False)
                expert(E - 1, False, True)
                turn(E - 1, NI - 1)
                down(E - 1, NI - 1)

            @block.scalar
            def _(act):
                def split_shared(c, par):
                    at = slice(c, c + 1) if isinstance(c, int) else bass.ds(c, 1)
                    act.wait_ge(s_in, (c + 1) * 32)
                    if not isinstance(c, int):
                        act.wait_ge(su_ps, 2 * (c - 1))
                    act.activation(sguh[:, par], s_raw[:, :, :, :], ACT.Copy).then_inc(sgu_hi, 1)
                    act.wait_ge(sd_in, (c + 1) * 16)
                    act.activation(sdh[:, at, :].rearrange("p a n -> p (a n)"), sd_raw[:, :], ACT.Copy).then_inc(sd_hi, 1)

                def gelu_shared(c):
                    for half in range(2):
                        act.wait_ge(sg_ps, 2 * c + half + 1)
                        if not isinstance(c, int) or c:
                            act.wait_ge(hs_ready, 2 * c + half - 1)
                        act.activation(gelu_s[:, half, :], ps[:, 2 * half, :], ACT.Gelu).then_inc(s_gelu, 1)

                act.wait_ge(var_done, 1)
                act.activation(rstd[:, :], rstd[:, :], ACT.Sqrt).then_inc(std_done, 1)
                act.wait_ge(gate_in, 16)
                act.activation(gateh[:, :, :], gate_raw[:, :, :], ACT.Copy).then_inc(gate_hi, 1)
                split_shared(0, 0)
                with act.Fori(0, G // 2) as gg:
                    for h_ in range(2):
                        g = gg * 2 + h_
                        act.wait_ge(xt_ps, g + 1)
                        act.activation(xth[:, :, bass.ds(g * P, P)], ps[:, h_, :].rearrange("p (k n) -> p k n", k=KD), ACT.Copy).then_inc(xt_hi, 1)
                act.wait_ge(shifted, 1)
                act.activation(route[:, :, :], route[:, :, :], ACT.Exp).then_inc(exp_done, 1)
                split_shared(1, 1)
                gelu_shared(0)
                with act.Fori(1, KI // 2) as cc:
                    split_shared(cc * 2, 0)
                    gelu_shared(cc * 2 - 1)
                    split_shared(cc * 2 + 1, 1)
                    gelu_shared(cc * 2)
                gelu_shared(KI - 1)
                act.wait_ge(hs_ready, 2 * KI)

                def step(gg):
                    for h_ in range(2):
                        g = gg * 2 + h_
                        if not isinstance(gg, int):
                            act.wait_ge(down_ps, g - 1)
                        act.activation(hsh[h_][:, :, :], hs[:, :, bass.ds(g * P, P)], ACT.Copy).then_inc(hs_hi, 1)

                steps(act, G // 2, step)

                def gelu_expert(e, n):
                    act.wait_ge(g_ps, e * NI + n + 1)
                    if not (isinstance(e, int) and e == 0 and n < 2):
                        act.wait_ge(h_ready, e * NI + n - 1)
                    act.activation(gelu_e[:, n % 2, :], ps[:, n % 2 * 2, :], ACT.Gelu).then_inc(e_gelu, 1)

                def turned_rows(e):
                    act.wait_ge(xgt_ps, e + 1)
                    act.wait_ge(u_ps, e * NI)
                    act.activation(xgth[:, :, :], ps[:, 6, :].rearrange("p (k n) -> p k n", k=KD), ACT.Copy).then_inc(xgt_hi, 1)

                def split_expert(e, n):
                    for a, used in ((0, g_ps), (1, u_ps)):
                        act.wait_ge(slot_in[n][a], (e + 1) * 16)
                        if not (isinstance(e, int) and e == 0 and n < 2):
                            act.wait_ge(used, e * NI + n - 1)
                        act.activation(weh[:, a, n % 2], slots[:, n, a], ACT.Copy).then_inc(we_hi, 1)

                def expert(e, last):
                    for n in range(NI):
                        if n < NI - 1:
                            split_expert(e, n + 1)
                        elif not last:
                            split_expert(e + 1, 0)
                        gelu_expert(e, n)
                    if not last:
                        turned_rows(e + 1)

                act.wait_ge(su_ps, 2 * KI)
                split_expert(0, 0)
                act.wait_ge(y_ready, G)
                turned_rows(0)
                expert(0, False)
                with act.Fori(1, E - 1) as e:
                    expert(e, False)
                expert(E - 1, True)

            @block.vector
            def _(dve):
                for g in range(G):
                    dve.bn_aggr(mv[:, g, :], stats[:, g, :]).then_inc(mv_done, 1)
                dve.wait_ge(mv_done, G)
                dve.tensor_scalar(rstd[:, :], mv[:, :, 1], EPS, None, ALU.add).then_inc(var_done, 1)
                dve.wait_ge(std_done, 1)
                dve.reciprocal(rstd[:, :], rstd[:, :]).then_inc(rstd_done, 1)
                dve.wait_ge(rstd_done, 1)

                def center(gg, h_):
                    g = gg * 2 + h_
                    if not isinstance(gg, int):
                        dve.wait_ge(xn_out[h_], gg * 16)
                    at = slice(g, g + 1) if isinstance(g, int) else bass.ds(g, 1)
                    dve.tensor_scalar(xn[:, h_, :], x[:, at, :].rearrange("p a n -> p (a n)"), mv[:, at, 0], rstd[:, at], ALU.subtract, ALU.mult).then_inc(xn_ready, 1)

                def turned(gg, h_):
                    g = gg * 2 + h_
                    dve.wait_ge(xt_hi, g + 1)
                    at = slice(g * P, g * P + P) if isinstance(g, int) else bass.ds(g * P, P)
                    dve.tensor_tensor(xtl[:, :, at], ps[:, h_, :].rearrange("p (k n) -> p k n", k=KD), xth[:, :, at].bitcast(F32), ALU.subtract).then_inc(xt_lo, 1)

                center(0, 0)
                center(0, 1)
                with dve.Fori(0, G // 2 - 1) as gg:
                    for h_ in range(2):
                        turned(gg, h_)
                        center(gg + 1, h_)
                turned(G // 2 - 1, 0)
                turned(G // 2 - 1, 1)
                dve.wait_ge(logit_ps, 1)
                dve.tensor_copy(score[:, :], ps[0:E, 4:6, :].rearrange("p a n -> p (a n)")).then_inc(logit_copied, 1)
                dve.wait_ge(logit_turned, 1)
                logits = ps[:, 7, 0:G * E].rearrange("p (g e) -> p g e", g=G)
                wide = lambda t: t[:, :].rearrange("p (g a) -> p g a", a=1).to_broadcast([P, G, E])
                dve.tensor_reduce(peak[:, :], logits, AX_X, ALU.max).then_inc(peak_done, 1)
                dve.wait_ge(peak_done, 1)
                dve.tensor_tensor(route[:, :, :], logits, wide(peak), ALU.subtract).then_inc(shifted, 1)
                dve.wait_ge(exp_done, 1)
                dve.tensor_reduce(total[:, :], route[:, :, :], AX_X, ALU.add).then_inc(sum_done, 1)
                dve.wait_ge(sum_done, 1)
                dve.reciprocal(total[:, :], total[:, :]).then_inc(inv_done, 1)
                dve.wait_ge(inv_done, 1)
                dve.tensor_tensor(route[:, :, :], route[:, :, :], wide(total), ALU.mult).then_inc(route_ready, 1)

                def gated(c, half):
                    dve.wait_ge(s_gelu, 2 * c + half + 1)
                    dve.wait_ge(su_ps, 2 * c + half + 1)
                    at = slice(c, c + 1) if isinstance(c, int) else bass.ds(c, 1)
                    dve.tensor_tensor(hs[:, at, half * 512:(half + 1) * 512].rearrange("p a n -> p (a n)"), gelu_s[:, half, :], ps[:, 2 * half + 1, :], ALU.mult).then_inc(hs_ready, 1)

                def pick(r):
                    dve.wait_ge(removed, r)
                    dve.memset(stand[:, :], 0.0)
                    dve.max(best8[:, :], score[:, :]).then_inc(found, 1)
                    dve.wait_ge(found, 2 * r + 1)
                    dve.memset(stand[:, :], 0.0)
                    dve.max_index(best8_at[:, :], best8[:, :], score[:, :]).then_inc(found, 1)
                    dve.wait_ge(found, 2 * r + 2)
                    dve.tensor_copy(best[:, bass.ds(r * 8, 8)], best8[:, :]).then_inc(placed, 1)
                    dve.tensor_copy(best_at[:, bass.ds(r * 8, 8)], best8_at[:, :]).then_inc(placed, 1)
                    dve.wait_ge(placed, 2 * r + 2)
                    dve.memset(stand[:, :], 0.0)
                    dve.match_replace(score[:, :], best8[:, :], score[:, :], -1.0).then_inc(removed, 1)

                gated(0, 0)
                gated(0, 1)
                dve.wait_ge(turn_ps, 1)
                dve.tensor_copy(score[:, :], ps[0:E, 4:6, :].rearrange("p a n -> p (a n)")).then_inc(score_ready, 1)
                dve.wait_ge(score_ready, 1)
                pick(0)
                pick(1)

                def pick_and_gate(c):
                    pick(c * 2)
                    gated(c, 0)
                    pick(c * 2 + 1)
                    gated(c, 1)

                with dve.Fori(1, KI) as c:
                    pick_and_gate(c)
                dve.wait_ge(picked_ps, 1)
                dve.tensor_copy(weight[:, :], ps[:, 5, 0:E]).then_inc(token_ready, 1)
                dve.tensor_copy(token[:, :], ps[:, 5, E:2 * E]).then_inc(token_ready, 1)
                def step(gg):
                    for h_ in range(2):
                        g = gg * 2 + h_
                        dve.wait_ge(hs_hi, g + 1)
                        dve.tensor_tensor(hsl[h_][:, :, :], hs[:, :, bass.ds(g * P, P)], hsh[h_][:, :, :].bitcast(F32), ALU.subtract).then_inc(hs_lo, 1)
                        dve.wait_ge(y_out[h_], gg * 16)
                        dve.wait_ge(down_ps, g + 1)
                        dve.tensor_tensor(y[:, h_, :], x[:, bass.ds(g, 1), :].rearrange("p a n -> p (a n)"), ps[:, 6 + h_, :], ALU.add).then_inc(y_ready, 1)
                steps(dve, G // 2, step)

                def gate_times_up(e, n):
                    dve.wait_ge(e_gelu, e * NI + n + 1)
                    dve.wait_ge(u_ps, e * NI + n + 1)
                    if not (isinstance(e, int) and e == 0 and n < 2):
                        dve.wait_ge(ht_ps, e * NI + n - 1)
                    dve.tensor_tensor(h[:, n % 2, :], gelu_e[:, n % 2, :], ps[:, n % 2 * 2 + 1, :], ALU.mult).then_inc(h_ready, 1)

                def turned_hidden(e, n):
                    dve.wait_ge(ht_ps, e * NI + n + 1)
                    if not (isinstance(e, int) and e == 0 and n < 2):
                        dve.wait_ge(d_used, e * NI + n - 1)
                    dve.tensor_copy(ht[:, n % 2], ps[:, 4, :].rearrange("p (k n) -> p k n", k=4)).then_inc(ht_ready, 1)

                def split_expert(e, n):
                    for a in range(2):
                        dve.wait_ge(we_hi, 2 * (e * NI + n) + a + 1)
                        dve.tensor_tensor(wel[:, a, n % 2], slots[:, n, a], weh[:, a, n % 2].bitcast(F32), ALU.subtract).then_inc(we_lo, 1)

                def turned_rows(e):
                    dve.wait_ge(xgt_hi, e + 1)
                    dve.tensor_tensor(xgtl[:, :, :], ps[:, 6, :].rearrange("p (k n) -> p k n", k=KD), xgth[:, :, :].bitcast(F32), ALU.subtract).then_inc(xgt_ready, 1)

                def weigh(e):
                    dve.wait_ge(d_used, (e + 1) * NI)
                    dve.wait_ge(scattered, e * 16)
                    at = slice(e, e + 1) if isinstance(e, int) else bass.ds(e, 1)
                    dve.tensor_scalar(eo[:, :], ps[:, 5, :], weight[:, at], None, ALU.mult).then_inc(eo_ready, 1)

                def expert(e, first, last):
                    for n in range(NI):
                        if n < NI - 1:
                            split_expert(e, n + 1)
                        elif not last:
                            split_expert(e + 1, 0)
                        if n == 0 and not first:
                            weigh(e - 1)
                        gate_times_up(e, n)
                        if n == NI - 1 and not last:
                            turned_rows(e + 1)
                        turned_hidden(e, n)

                dve.wait_ge(hs_lo, G)
                split_expert(0, 0)
                turned_rows(0)
                dve.wait_ge(token_ready, 2)
                dve.wait_ge(y_ready, G)
                expert(0, True, False)
                expert(1, False, False)
                with dve.Fori(2, E - 1) as e:
                    expert(e, False, False)
                expert(E - 1, False, True)
                weigh(E - 1)

            @block.gpsimd
            def _(pool):
                def split_shared(c, par):
                    at = slice(c, c + 1) if isinstance(c, int) else bass.ds(c, 1)
                    pool.wait_ge(sgu_hi, c + 1)
                    pool.tensor_tensor(sgul[:, par], s_raw[:, :, :, :], sguh[:, par].bitcast(F32), ALU.subtract).then_inc(sgu_lo, 1)
                    pool.wait_ge(sd_hi, c + 1)
                    pool.tensor_tensor(sdl[:, at, :].rearrange("p a n -> p (a n)"), sd_raw[:, :], sdh[:, at, :].rearrange("p a n -> p (a n)").bitcast(F32), ALU.subtract).then_inc(sd_lo, 1)

                pool.wait_ge(gate_hi, 1)
                pool.tensor_tensor(gatel[:, :, :], gate_raw[:, :, :], gateh[:, :, :].bitcast(F32), ALU.subtract).then_inc(gate_lo, 1)
                split_shared(0, 0)
                split_shared(1, 1)
                with pool.Fori(1, KI // 2) as cc:
                    split_shared(cc * 2, 0)
                    split_shared(cc * 2 + 1, 1)

                def gather(e):
                    at = slice(e, e + 1) if isinstance(e, int) else bass.ds(e, 1)
                    pool.wait_ge(gathered, e * 16)
                    pool.tensor_copy(gather_at[:, :], token[:, at]).then_inc(gather_idx, 1)
                    pool.wait_ge(gather_idx, e + 1)
                    pool.wait_ge(xgt_ps, e)
                    pool.tensor_tensor(pool_stand[:, :], ident[:, 0:1], ident[:, 0:1], ALU.mult)
                    pool.indirect_dma_start(xg[:, :], None, xn_dram[:, :], bass.IndirectOffsetOnAxis(gather_at[:, 0:1], 0)).then_inc(gathered, 16)

                def scatter(e):
                    at = slice(e, e + 1) if isinstance(e, int) else bass.ds(e, 1)
                    pool.wait_ge(scattered, e * 16)
                    pool.tensor_copy(scatter_at[:, :], token[:, at]).then_inc(scatter_idx, 1)
                    pool.wait_ge(scatter_idx, e + 1)
                    pool.wait_ge(eo_ready, e + 1)
                    pool.tensor_tensor(pool_stand[:, :], ident[:, 0:1], ident[:, 0:1], ALU.mult)
                    pool.indirect_dma_start(out[:, :], bass.IndirectOffsetOnAxis(scatter_at[:, 0:1], 0), eo[:, :], None, compute_op=ALU.add).then_inc(scattered, 16)

                pool.wait_ge(token_ready, 2)
                for n in range(2):
                    pool.wait_ge(xn_out[n], G // 2 * 16)
                gather(0)
                for n in range(2):
                    pool.wait_ge(y_out[n], G // 2 * 16)
                def step(e):
                    gather(e + 1)
                    scatter(e)
                steps(pool, E - 1, step)
                scatter(E - 1)


def perceiver_block(nc, x_dram, ctxT, ctx, mask, wq_x, wkT_x, wv_x, wo_x, bo_x, wq, wk, wv, wo, rel_bias, onehot,
                    gate, sg, su, sd, wg, wu, wd, ident_dram, rows_dram, out):
    ps = nc.alloc_psum_tensor("ps", [P, 8, 512], F32)
    xn_dram = nc.dram_tensor("layernormed", [T, D], F32, kind="Internal").ap()
    sb = Map(nc, (nc.sbuf_base + 63) // 64 * 64)
    x_at = sb.offset
    x, ident = sb("x", [P, G, D], F32), sb("ident", [P, P], F32)
    stats = sb("stats", [P, G, 6], F32)
    cross_attention(nc, ps, x_dram.rearrange("b s d -> (b s) d"), ctxT, ctx, mask, wq_x, wkT_x, wv_x, wo_x, bo_x,
                    ident_dram, rows_dram, x, ident, stats, sb.offset)
    xth, xtl = sb("all_xth", [P, KD, T], F32R), sb("all_xtl", [P, KD, T], F32R)
    self_attention(nc, ps, wq, wk, wv, wo, rel_bias, onehot, x, ident, stats, xth, xtl, sb.offset)
    mixture(nc, ps, gate, sg, su, sd, wg, wu, wd, xn_dram, out.rearrange("b s d -> (b s) d"), x, ident, stats, xth, xtl, x_at, sb.offset)


def bucket_onehot():
    distance = np.arange(S)[None, :] - np.arange(S)[:, None]
    half, exact, furthest = NBUCKET // 2, NBUCKET // 4, 128
    near = np.abs(distance)
    scale = np.float32(math.log(furthest / exact))
    far = exact + (np.log(np.maximum(near, 1).astype(np.float32) / np.float32(exact)) / scale * np.float32(half - exact)).astype(np.int32)
    bucket = (distance > 0) * half + np.where(near < exact, near, np.minimum(far, half - 1))
    onehot = np.zeros((NBUCKET, S, BPG, S), np.float32)
    for i in range(S):
        for j in range(S):
            onehot[bucket[i, j], j, :, i] = 1
    return onehot.reshape(NBUCKET, S * P)


def kernel(**inputs):
    import concourse.bacc as bacc
    from concourse.bass_utils import run_bass_kernel_spmd

    a = {k: np.asarray(v) for k, v in inputs.items()}
    w = lambda name: a["L0_" + name]
    columns = lambda t: t.reshape(KI, P, KD, P).transpose(0, 3, 2, 1)
    expert_columns = lambda t: t.reshape(E, NI, 512, KD, P).transpose(0, 1, 4, 3, 2)
    arrays = {
        "x": a["x"],
        "ctxT": a["ctx_768"].transpose(0, 2, 1),
        "ctx": a["ctx_768"],
        "mask": a["mask_BxS2_bk0"],
        "xattn_wq": w("xattn_W_q"), "xattn_wkT": w("xattn_W_k").T, "xattn_wv": w("xattn_W_v"), "xattn_wo": w("xattn_W_o"), "xattn_bo": w("xattn_b_o"),
        "attn_wq": w("attn_wq"), "attn_wk": w("attn_wk"), "attn_wv": w("attn_wv"), "attn_wo": w("attn_wo"), "rel_bias": w("attn_rel_bias"),
        "onehot": bucket_onehot(),
        "gate": w("ffn_gate_w").T,
        "sg": columns(w("ffn_Sg")), "su": columns(w("ffn_Su")), "sd": w("ffn_Sd").T,
        "wg": expert_columns(w("ffn_Wg")), "wu": expert_columns(w("ffn_Wu")),
        "wd": w("ffn_Wd").reshape(E, D, NI, 4, P).transpose(0, 2, 4, 3, 1),
        "ident": np.eye(P, dtype=np.float32),
        "rows": np.array([[0, 0], [-1, 0], [0, -1], [-1, -1]], np.float32),
    }
    arrays = {"in_" + k: np.ascontiguousarray(v) for k, v in arrays.items()}
    nc = bacc.Bacc("TRN2", target_bir_lowering=False, num_devices=1)
    args = [nc.dram_tensor(k, v.shape, mybir.dt.from_np(v.dtype), kind="ExternalInput").ap() for k, v in arrays.items()]
    out = nc.dram_tensor("out", [B, S, D], F32, kind="ExternalOutput").ap()
    perceiver_block(nc, *args, out)
    result = run_bass_kernel_spmd(nc, [arrays], core_ids=[0])
    return result.results[0]["out"]
```
